# Optimizing a Trainium2 kernel written in Bass

```python
import numpy as np
import jax
import jax.numpy as jnp

def _softmax(x, axis=-1):
    return jax.nn.softmax(x, axis=axis)

def _gelu(x):
    return jax.nn.gelu(x, approximate=True)

def _silu(x):
    return jax.nn.silu(x)

def _sigmoid(x):
    return jax.nn.sigmoid(x)

def _layernorm(x, axis=-1, eps=1e-05):
    m = jnp.mean(x, axis=axis, keepdims=True)
    v = jnp.var(x, axis=axis, keepdims=True)
    return (x - m) / jnp.sqrt(v + eps)

def _scatter_add(tgt, idx, src, axis=0):
    return tgt.at[idx].add(src)

def _segment_sum(src, seg, n):
    return jax.ops.segment_sum(src, seg, n)
kernel_name = 'mk_audio_tower_d4_tok_audfeat256_r4_b0c743'

def setup_inputs(seed: int=0):
    np.random.seed(seed)
    _w = jnp.asarray

    def _rec_inputs():
        import jax
        import jax.numpy as jnp
        _rk = jax.random.key(seed)
        x = 7.22013e-05 + 1.00017 * jax.random.normal(jax.random.fold_in(_rk, 1), (32, 250, 64), jnp.float32)
        return x
    x = _rec_inputs()

    def _L0_tok_setup():
        import jax, jax.numpy as jnp
        import numpy as np
        WIN = 9
        key = jax.random.key(seed)
        ks = jax.random.split(key, 4)
        N, L, C, U = (8, 1024, 64, 64)
        x = jax.random.normal(ks[0], (N, L, C), dtype=jnp.float32)
        W_qry = jax.random.normal(ks[1], (C, U), dtype=jnp.float32) * 0.05
        W_key = jax.random.normal(ks[2], (C, U), dtype=jnp.float32) * 0.05
        v = jax.random.normal(ks[3], (U,), dtype=jnp.float32) * 0.05
        b = jnp.zeros((U,), dtype=jnp.float32)
        return {'x': x, 'W_qry': W_qry, 'W_key': W_key, 'v': v, 'b': b}
    _L0_tok_all = _L0_tok_setup()
    _L0_tok_in = {k: v for k, v in _L0_tok_all.items() if k in ('W_qry', 'W_key', 'v', 'b')}
    del _L0_tok_all

    def _L0_attn_setup():
        import jax, jax.numpy as jnp
        import numpy as np
        key = jax.random.key(seed)
        ks = jax.random.split(key, 5)
        b, t, e, h = (8, 256, 64, 8)
        w = lambda k, shape: jax.random.normal(k, shape, dtype=jnp.float32) * 0.02
        return {'x': jax.random.normal(ks[0], (b, t, e), dtype=jnp.float32), 'Wq': w(ks[1], (e, e * h)), 'bq': jnp.zeros((e * h,), jnp.float32), 'Wk': w(ks[2], (e, e * h)), 'bk': jnp.zeros((e * h,), jnp.float32), 'Wv': w(ks[3], (e, e * h)), 'bv': jnp.zeros((e * h,), jnp.float32), 'Wu': w(ks[4], (e * h, e)), 'bu': jnp.zeros((e,), jnp.float32)}
    _L0_attn_all = _L0_attn_setup()
    _L0_attn_in = {k: v for k, v in _L0_attn_all.items() if k in ('Wq', 'bq', 'Wk', 'bk', 'Wv', 'bv', 'Wu', 'bu')}
    del _L0_attn_all

    def _L0_ffn_setup():
        import jax, jax.numpy as jnp
        import numpy as np
        B, S, D = (8, 1024, 64)
        H = 4 * D
        CAPACITY = 0.5
        key = jax.random.key(seed)
        ks = jax.random.split(key, 6)
        x = jax.random.normal(ks[0], (B, S, D), dtype=jnp.float32)
        attention_mask = jnp.zeros((B, 1, 1, S), dtype=jnp.float32)
        wr = jax.random.normal(ks[1], (D, 1), dtype=jnp.float32) * 0.02
        br = jnp.zeros((1,), dtype=jnp.float32)
        w1 = jax.random.normal(ks[2], (D, H), dtype=jnp.float32) * 0.02
        b1 = jnp.zeros((H,), dtype=jnp.float32)
        w2 = jax.random.normal(ks[3], (H, D), dtype=jnp.float32) * 0.02
        b2 = jnp.zeros((D,), dtype=jnp.float32)
        return {'x': x, 'attention_mask': attention_mask, 'wr': wr, 'br': br, 'w1': w1, 'b1': b1, 'w2': w2, 'b2': b2}
    _L0_ffn_all = _L0_ffn_setup()
    _L0_ffn_in = {k: v for k, v in _L0_ffn_all.items() if k in ('attention_mask', 'wr', 'br', 'w1', 'b1', 'w2', 'b2')}
    del _L0_ffn_all

    def _L1_attn_setup():
        import jax, jax.numpy as jnp
        import numpy as np
        import math
        B, T, D_MODEL = (1, 512, 64)
        N_Q, N_KV = (16, 1)
        D_HEAD = D_MODEL // N_KV
        QPG = N_Q // N_KV
        ROPE_BASE = 10000.0
        WINDOW = 128
        EPS = 1.1920929e-07
        NEG = -1e+30

        def _rope(x, base=ROPE_BASE):
            t, d = (x.shape[-2], x.shape[-1])
            freqs = base ** (-2.0 * jnp.arange(d // 2, dtype=jnp.float32) / d)
            theta = jnp.arange(t, dtype=jnp.float32)[:, None] * freqs[None, :]
            cos, sin = (jnp.cos(theta), jnp.sin(theta))
            x1, x2 = (x[..., 0::2], x[..., 1::2])
            r1 = x1 * cos - x2 * sin
            r2 = x1 * sin + x2 * cos
            return jnp.stack([r1, r2], axis=-1).reshape(x.shape)

        def _rmsnorm(x, w):
            return x * jax.lax.rsqrt(jnp.mean(x * x, axis=-1, keepdims=True) + EPS) * w
        key = jax.random.key(seed)
        k0, k1, k2, k3 = jax.random.split(key, 4)
        x = jax.random.normal(k0, (B, T, D_MODEL), dtype=jnp.float32)
        wq = jax.random.normal(k1, (QPG * N_KV * D_HEAD, D_MODEL), dtype=jnp.float32) * 0.02
        wkv = jax.random.normal(k2, (2 * D_HEAD * N_KV, D_MODEL), dtype=jnp.float32) * 0.02
        wo = jax.random.normal(k3, (D_MODEL, D_HEAD * N_Q * N_KV), dtype=jnp.float32) * 0.02
        q_norm_w = jnp.ones((D_HEAD,), dtype=jnp.float32)
        k_norm_w = jnp.ones((D_HEAD,), dtype=jnp.float32)
        return {'x': x, 'wq': wq, 'wkv': wkv, 'wo': wo, 'q_norm_w': q_norm_w, 'k_norm_w': k_norm_w}
    _L1_attn_all = _L1_attn_setup()
    _L1_attn_in = {k: v for k, v in _L1_attn_all.items() if k in ('wq', 'wkv', 'wo', 'q_norm_w', 'k_norm_w')}
    del _L1_attn_all

    def _L1_ffn_setup():
        import jax, jax.numpy as jnp
        import numpy as np
        C = 64
        HID = 256
        E = 8
        TEMP = 1.0
        key = jax.random.key(seed)
        ks = jax.random.split(key, 7)
        x = jax.random.normal(ks[0], (8, 4096, C), dtype=jnp.float32)
        W1 = jax.random.normal(ks[1], (C, HID), dtype=jnp.float32) * 0.02
        b1 = jnp.zeros((HID,), dtype=jnp.float32)
        Wg = jax.random.normal(ks[2], (HID, E), dtype=jnp.float32) * 0.02
        bg = jnp.zeros((E,), dtype=jnp.float32)
        Wd = jax.random.normal(ks[3], (E, HID, C), dtype=jnp.float32) * 0.02
        bd = jnp.zeros((E, C), dtype=jnp.float32)
        return {'x': x, 'W1': W1, 'b1': b1, 'Wg': Wg, 'bg': bg, 'Wd': Wd, 'bd': bd}
    _L1_ffn_all = _L1_ffn_setup()
    _L1_ffn_in = {k: v for k, v in _L1_ffn_all.items() if k in ('W1', 'b1', 'Wg', 'bg', 'Wd', 'bd')}
    del _L1_ffn_all

    def _L2_attn_setup():
        import jax, jax.numpy as jnp
        import numpy as np
        B, N, D, H = (4, 256, 64, 8)
        key = jax.random.key(seed)
        k1, k2, k3 = jax.random.split(key, 3)
        x = jax.random.normal(k1, (B, N, D), dtype=jnp.float32)
        Wqkv = jax.random.normal(k2, (D, 3 * D * H), dtype=jnp.float32) * 0.02
        bqkv = jnp.zeros((3 * D * H,), dtype=jnp.float32)
        W0 = jax.random.normal(k3, (D * H, D), dtype=jnp.float32) * 0.02
        b0 = jnp.zeros((D,), dtype=jnp.float32)
        return {'x': x, 'Wqkv': Wqkv, 'bqkv': bqkv, 'W0': W0, 'b0': b0}
    _L2_attn_all = _L2_attn_setup()
    _L2_attn_in = {k: v for k, v in _L2_attn_all.items() if k in ('Wqkv', 'bqkv', 'W0', 'b0')}
    del _L2_attn_all

    def _L2_ffn_setup():
        import jax, jax.numpy as jnp
        import numpy as np
        DIM = 64
        HEADS = 8
        NUM_KEYS = 64
        NUM_KV = NUM_KEYS ** 2
        PK_TOPK = 16
        FINAL_TOPK = 16
        DIM_KEY = DIM // 2
        P = 2

        def _pk(x, Wq_pk, pk_keys):
            b, n, _ = x.shape
            q = (x @ Wq_pk).reshape(b, n, P, HEADS, DIM_KEY).transpose(2, 0, 1, 3, 4)
            sim = jnp.einsum('pbnhd,pkhd->pbnhk', q, pk_keys)
            scores, idx = jax.lax.top_k(sim, PK_TOPK)
            idx0 = idx[0]
            idx1 = idx[1] * NUM_KEYS
            index = (idx0[..., :, None] + idx1[..., None, :]).reshape(b, n, HEADS, PK_TOPK * PK_TOPK)
            score = (scores[0][..., :, None] + scores[1][..., None, :]).reshape(b, n, HEADS, PK_TOPK * PK_TOPK)
            final_scores, pk_idx = jax.lax.top_k(score, FINAL_TOPK)
            final_indices = jnp.take_along_axis(index, pk_idx, axis=-1)
            final_scores = jax.nn.softmax(final_scores, axis=-1)
            return (final_scores, final_indices)
        key = jax.random.key(seed)
        ks = jax.random.split(key, 7)
        b, n = (2, 256)
        std = 0.02
        x = jax.random.normal(ks[0], (b, n, DIM), dtype=jnp.float32)
        Wq_pk = jax.random.normal(ks[1], (DIM, P * HEADS * DIM_KEY), dtype=jnp.float32) * std
        pk_keys = jax.random.normal(ks[2], (P, NUM_KEYS, HEADS, DIM_KEY), dtype=jnp.float32) * std
        Wq = jax.random.normal(ks[3], (DIM, HEADS * DIM), dtype=jnp.float32) * std
        keys_table = jax.random.normal(ks[4], (NUM_KV * HEADS, DIM), dtype=jnp.float32) * std
        values_table = jax.random.normal(ks[5], (NUM_KV * HEADS, DIM), dtype=jnp.float32) * std
        Wo = jax.random.normal(ks[6], (DIM * HEADS, DIM), dtype=jnp.float32) * std
        return {'x': x, 'Wq_pk': Wq_pk, 'pk_keys': pk_keys, 'Wq': Wq, 'keys_table': keys_table, 'values_table': values_table, 'Wo': Wo}
    _L2_ffn_all = _L2_ffn_setup()
    _L2_ffn_in = {k: v for k, v in _L2_ffn_all.items() if k in ('Wq_pk', 'pk_keys', 'Wq', 'keys_table', 'values_table', 'Wo')}
    del _L2_ffn_all

    def _L3_attn_setup():
        import jax, jax.numpy as jnp
        import numpy as np
        H, D = (8, 32)
        EPS = 1e-05
        key = jax.random.key(seed)
        ks = jax.random.split(key, 4)
        B, N, C = (2, 512, 64)
        inner = H * D
        return {'node_features': jax.random.normal(ks[0], (B, N, C), jnp.float32), 'ln_gamma': jnp.ones((C,), jnp.float32), 'ln_beta': jnp.zeros((C,), jnp.float32), 'W_qkv': jax.random.normal(ks[1], (3 * inner, C), jnp.float32) * 0.02, 'W_gate': jax.random.normal(ks[2], (inner, C), jnp.float32) * 0.02, 'b_gate': jnp.ones((inner,), jnp.float32), 'W_final': jax.random.normal(ks[3], (C, inner), jnp.float32) * 0.02, 'b_final': jnp.zeros((C,), jnp.float32)}
    _L3_attn_all = _L3_attn_setup()
    _L3_attn_in = {k: v for k, v in _L3_attn_all.items() if k in ('ln_gamma', 'ln_beta', 'W_qkv', 'W_gate', 'b_gate', 'W_final', 'b_final')}
    del _L3_attn_all

    def _L3_ffn_setup():
        import jax, jax.numpy as jnp
        import numpy as np
        B, N, D = (16, 1024, 64)
        NUM_EXPERTS, TOP_K, HEADS = (4, 2, 4)
        N_EDGES = 262144
        LN_EPS = 1e-05

        def _layernorm(x, g, b):
            mu = x.mean(-1, keepdims=True)
            var = ((x - mu) ** 2).mean(-1, keepdims=True)
            return (x - mu) * jax.lax.rsqrt(var + LN_EPS) * g + b

        def _forward(x, edge_index, W_gat, att_src, att_dst, b_gat, ln_gamma, ln_beta, W1, b1, W2, b2):
            Bc, Nc, Dc = x.shape
            M = Bc * Nc
            x_flat = x.reshape(M, Dc)
            h = (x_flat @ W_gat).reshape(M, HEADS, NUM_EXPERTS)
            loops = jnp.arange(M, dtype=edge_index.dtype)
            src = jnp.concatenate([edge_index[0], loops])
            dst = jnp.concatenate([edge_index[1], loops])
            a_src = (h * att_src).sum(-1)
            a_dst = (h * att_dst).sum(-1)
            e = jax.nn.leaky_relu(a_src[src] + a_dst[dst], negative_slope=0.2)
            e_max = jax.ops.segment_max(e, dst, num_segments=M)
            ee = jnp.exp(e - e_max[dst])
            denom = jax.ops.segment_sum(ee, dst, num_segments=M)
            alpha = ee / (denom[dst] + 1e-16)
            msg = h[src] * alpha[:, :, None]
            agg = jax.ops.segment_sum(msg, dst, num_segments=M).reshape(M, HEADS * NUM_EXPERTS) + b_gat
            scores = _layernorm(agg, ln_gamma, ln_beta).reshape(M, HEADS, NUM_EXPERTS).mean(1)
            scores = scores.reshape(Bc, Nc, NUM_EXPERTS)
            topk_s, topk_i = jax.lax.top_k(scores, TOP_K)
            w = jax.nn.softmax(topk_s, axis=-1)
            out = jnp.zeros_like(x)
            for ei in range(NUM_EXPERTS):
                g = jnp.where(topk_i == ei, w, 0.0).sum(-1)
                hh = jax.nn.gelu(x @ W1[ei] + b1[ei], approximate=False)
                out = out + g[..., None] * (hh @ W2[ei] + b2[ei])
            return out
        key = jax.random.key(seed)
        ks = jax.random.split(key, 8)
        s = 0.05
        return {'x': jax.random.normal(ks[0], (B, N, D), jnp.float32), 'W_gat': jax.random.normal(ks[1], (D, HEADS * NUM_EXPERTS), jnp.float32) * s, 'att_src': jax.random.normal(ks[2], (HEADS, NUM_EXPERTS), jnp.float32) * s, 'att_dst': jax.random.normal(ks[3], (HEADS, NUM_EXPERTS), jnp.float32) * s, 'b_gat': jnp.zeros((HEADS * NUM_EXPERTS,), jnp.float32), 'ln_gamma': jnp.ones((HEADS * NUM_EXPERTS,), jnp.float32), 'ln_beta': jnp.zeros((HEADS * NUM_EXPERTS,), jnp.float32), 'W1': jax.random.normal(ks[4], (NUM_EXPERTS, D, 2 * D), jnp.float32) * s, 'b1': jnp.zeros((NUM_EXPERTS, 2 * D), jnp.float32), 'W2': jax.random.normal(ks[5], (NUM_EXPERTS, 2 * D, D), jnp.float32) * s, 'b2': jnp.zeros((NUM_EXPERTS, D), jnp.float32), 'edge_index': jax.random.randint(ks[6], (2, N_EDGES), 0, B * N, jnp.int32)}
    _L3_ffn_all = _L3_ffn_setup()
    _L3_ffn_in = {k: v for k, v in _L3_ffn_all.items() if k in ('W_gat', 'att_src', 'att_dst', 'b_gat', 'ln_gamma', 'ln_beta', 'W1', 'b1', 'W2', 'b2', 'edge_index')}
    del _L3_ffn_all
    return {'x': x, 'L0_tok_W_qry': _L0_tok_in['W_qry'], 'L0_tok_W_key': _L0_tok_in['W_key'], 'L0_tok_v': _L0_tok_in['v'], 'L0_tok_b': _L0_tok_in['b'], 'L0_attn_Wq': _L0_attn_in['Wq'], 'L0_attn_bq': _L0_attn_in['bq'], 'L0_attn_Wk': _L0_attn_in['Wk'], 'L0_attn_bk': _L0_attn_in['bk'], 'L0_attn_Wv': _L0_attn_in['Wv'], 'L0_attn_bv': _L0_attn_in['bv'], 'L0_attn_Wu': _L0_attn_in['Wu'], 'L0_attn_bu': _L0_attn_in['bu'], 'L0_ffn_attention_mask': _L0_ffn_in['attention_mask'], 'L0_ffn_wr': _L0_ffn_in['wr'], 'L0_ffn_br': _L0_ffn_in['br'], 'L0_ffn_w1': _L0_ffn_in['w1'], 'L0_ffn_b1': _L0_ffn_in['b1'], 'L0_ffn_w2': _L0_ffn_in['w2'], 'L0_ffn_b2': _L0_ffn_in['b2'], 'L1_attn_wq': _L1_attn_in['wq'], 'L1_attn_wkv': _L1_attn_in['wkv'], 'L1_attn_wo': _L1_attn_in['wo'], 'L1_attn_q_norm_w': _L1_attn_in['q_norm_w'], 'L1_attn_k_norm_w': _L1_attn_in['k_norm_w'], 'L1_ffn_W1': _L1_ffn_in['W1'], 'L1_ffn_b1': _L1_ffn_in['b1'], 'L1_ffn_Wg': _L1_ffn_in['Wg'], 'L1_ffn_bg': _L1_ffn_in['bg'], 'L1_ffn_Wd': _L1_ffn_in['Wd'], 'L1_ffn_bd': _L1_ffn_in['bd'], 'L2_attn_Wqkv': _L2_attn_in['Wqkv'], 'L2_attn_bqkv': _L2_attn_in['bqkv'], 'L2_attn_W0': _L2_attn_in['W0'], 'L2_attn_b0': _L2_attn_in['b0'], 'L2_ffn_Wq_pk': _L2_ffn_in['Wq_pk'], 'L2_ffn_pk_keys': _L2_ffn_in['pk_keys'], 'L2_ffn_Wq': _L2_ffn_in['Wq'], 'L2_ffn_keys_table': _L2_ffn_in['keys_table'], 'L2_ffn_values_table': _L2_ffn_in['values_table'], 'L2_ffn_Wo': _L2_ffn_in['Wo'], 'L3_attn_ln_gamma': _L3_attn_in['ln_gamma'], 'L3_attn_ln_beta': _L3_attn_in['ln_beta'], 'L3_attn_W_qkv': _L3_attn_in['W_qkv'], 'L3_attn_W_gate': _L3_attn_in['W_gate'], 'L3_attn_b_gate': _L3_attn_in['b_gate'], 'L3_attn_W_final': _L3_attn_in['W_final'], 'L3_attn_b_final': _L3_attn_in['b_final'], 'L3_ffn_W_gat': _L3_ffn_in['W_gat'], 'L3_ffn_att_src': _L3_ffn_in['att_src'], 'L3_ffn_att_dst': _L3_ffn_in['att_dst'], 'L3_ffn_b_gat': _L3_ffn_in['b_gat'], 'L3_ffn_ln_gamma': _L3_ffn_in['ln_gamma'], 'L3_ffn_ln_beta': _L3_ffn_in['ln_beta'], 'L3_ffn_W1': _L3_ffn_in['W1'], 'L3_ffn_b1': _L3_ffn_in['b1'], 'L3_ffn_W2': _L3_ffn_in['W2'], 'L3_ffn_b2': _L3_ffn_in['b2'], 'L3_ffn_edge_index': _L3_ffn_in['edge_index']}

def reference(x, L0_tok_W_qry, L0_tok_W_key, L0_tok_v, L0_tok_b, L0_attn_Wq, L0_attn_bq, L0_attn_Wk, L0_attn_bk, L0_attn_Wv, L0_attn_bv, L0_attn_Wu, L0_attn_bu, L0_ffn_attention_mask, L0_ffn_wr, L0_ffn_br, L0_ffn_w1, L0_ffn_b1, L0_ffn_w2, L0_ffn_b2, L1_attn_wq, L1_attn_wkv, L1_attn_wo, L1_attn_q_norm_w, L1_attn_k_norm_w, L1_ffn_W1, L1_ffn_b1, L1_ffn_Wg, L1_ffn_bg, L1_ffn_Wd, L1_ffn_bd, L2_attn_Wqkv, L2_attn_bqkv, L2_attn_W0, L2_attn_b0, L2_ffn_Wq_pk, L2_ffn_pk_keys, L2_ffn_Wq, L2_ffn_keys_table, L2_ffn_values_table, L2_ffn_Wo, L3_attn_ln_gamma, L3_attn_ln_beta, L3_attn_W_qkv, L3_attn_W_gate, L3_attn_b_gate, L3_attn_W_final, L3_attn_b_final, L3_ffn_W_gat, L3_ffn_att_src, L3_ffn_att_dst, L3_ffn_b_gat, L3_ffn_ln_gamma, L3_ffn_ln_beta, L3_ffn_W1, L3_ffn_b1, L3_ffn_W2, L3_ffn_b2, L3_ffn_edge_index):
    import jax
    import jax.numpy as jnp

    def _L0_tok_ref(x, W_qry, W_key, v, b):
        import jax, jax.numpy as jnp
        import numpy as np
        WIN = 9
        N, L, C = x.shape
        n_w = L - WIN + 1
        idx = jnp.arange(n_w)[:, None] + jnp.arange(WIN)[None, :]
        x_win = x[:, idx]
        x_ctr = x[:, WIN // 2:WIN // 2 + n_w]
        key = jnp.einsum('nwsc,cu->nwsu', x_win, W_key)
        qry = jnp.einsum('nwc,cu->nwu', x_ctr, W_qry)
        score = jnp.einsum('nwsu,u->nws', jnp.tanh(qry[:, :, None, :] + key + b), v)
        weight = jax.nn.softmax(score, axis=2)
        out = jnp.einsum('nwsc,nws->nwc', x_win, weight)
        return out

    def _L0_attn_ref(x, Wq, bq, Wk, bk, Wv, bv, Wu, bu):
        import jax, jax.numpy as jnp
        import numpy as np
        b, t, e = x.shape
        h = Wq.shape[1] // e
        q = (x @ Wq + bq).reshape(b, t, h, e)
        k = (x @ Wk + bk).reshape(b, t, h, e)
        v = (x @ Wv + bv).reshape(b, t, h, e)
        scores = jnp.einsum('bihe,bjhe->bhij', q, k) / jnp.sqrt(jnp.asarray(e, jnp.float32))
        i = jnp.arange(t)[:, None]
        j = jnp.arange(t)[None, :]
        scores = jnp.where(j >= i, -jnp.inf, scores)
        scores = jnp.where(i == 0, 0.0, scores)
        att = jax.nn.softmax(scores, axis=-1)
        att = jnp.where(i == 0, 0.0, att)
        out = jnp.einsum('bhij,bjhe->bihe', att, v).reshape(b, t, h * e)
        return out @ Wu + bu

    def _L0_ffn_ref(x, attention_mask, wr, br, w1, b1, w2, b2):
        import jax, jax.numpy as jnp
        import numpy as np
        B, S, D = (8, 1024, 64)
        H = 4 * D
        CAPACITY = 0.5
        b, s, d = x.shape
        weights = (jnp.einsum('bsd,do->bso', x, wr) + br)[..., 0]
        k = max(1, int(CAPACITY * s))
        kk = k - 1 if k > 1 else 1
        _, idx = jax.lax.top_k(weights, k)
        sel_idx = idx[:, :kk]
        sel = jnp.take_along_axis(x, sel_idx[:, :, None], axis=1)
        h = jax.nn.gelu(jnp.einsum('bkd,dh->bkh', sel, w1) + b1)
        y = jnp.einsum('bkh,hd->bkd', h, w2) + b2
        w_sel = jnp.take_along_axis(weights, sel_idx, axis=1)
        y = y * w_sel[..., None]
        batch_idx = jnp.arange(b)[:, None]
        processed = jnp.zeros_like(x).at[batch_idx, sel_idx].set(y)
        return processed + x

    def _L1_attn_ref(x, wq, wkv, wo, q_norm_w, k_norm_w):
        import jax, jax.numpy as jnp
        import numpy as np
        import math
        B, T, D_MODEL = (1, 512, 64)
        N_Q, N_KV = (16, 1)
        D_HEAD = D_MODEL // N_KV
        QPG = N_Q // N_KV
        ROPE_BASE = 10000.0
        WINDOW = 128
        EPS = 1.1920929e-07
        NEG = -1e+30

        def _rope(x, base=ROPE_BASE):
            t, d = (x.shape[-2], x.shape[-1])
            freqs = base ** (-2.0 * jnp.arange(d // 2, dtype=jnp.float32) / d)
            theta = jnp.arange(t, dtype=jnp.float32)[:, None] * freqs[None, :]
            cos, sin = (jnp.cos(theta), jnp.sin(theta))
            x1, x2 = (x[..., 0::2], x[..., 1::2])
            r1 = x1 * cos - x2 * sin
            r2 = x1 * sin + x2 * cos
            return jnp.stack([r1, r2], axis=-1).reshape(x.shape)

        def _rmsnorm(x, w):
            return x * jax.lax.rsqrt(jnp.mean(x * x, axis=-1, keepdims=True) + EPS) * w
        Bx, Tx, C = x.shape
        q = x @ wq.T
        kv = x @ wkv.T
        k, v = (kv[..., :N_KV * D_HEAD], kv[..., N_KV * D_HEAD:])
        q = q.reshape(Bx, Tx, QPG, N_KV, D_HEAD).transpose(0, 2, 3, 1, 4)
        k = k.reshape(Bx, Tx, 1, N_KV, D_HEAD).transpose(0, 2, 3, 1, 4)
        v = v.reshape(Bx, Tx, 1, N_KV, D_HEAD).transpose(0, 2, 3, 1, 4)
        q = _rmsnorm(_rope(q), q_norm_w)
        k = _rmsnorm(_rope(k), k_norm_w)
        rows = jnp.arange(Tx)[:, None]
        cols = jnp.arange(Tx)[None, :]
        mask = (cols <= rows) & (rows - cols <= WINDOW)
        scale = 1.0 / math.sqrt(D_HEAD)
        scores = jnp.einsum('bqgtd,bqgsd->bqgts', q, k) * scale
        scores = jnp.where(mask[None, None, None], scores, NEG)
        attn = jax.nn.softmax(scores, axis=-1)
        out = jnp.einsum('bqgts,bqgsd->bqgtd', attn, v)
        out = out.transpose(0, 3, 1, 2, 4).reshape(Bx, Tx, QPG * N_KV * D_HEAD)
        return out @ wo.T

    def _L1_ffn_ref(x, W1, b1, Wg, bg, Wd, bd):
        import jax, jax.numpy as jnp
        import numpy as np
        C = 64
        HID = 256
        E = 8
        TEMP = 1.0
        orig_shape = x.shape
        xf = x.reshape(-1, orig_shape[-1])
        H = jax.nn.gelu(xf @ W1 + b1, approximate=False)
        probs = jax.nn.softmax((H @ Wg + bg) / TEMP, axis=-1)
        assign = jnp.argmax(probs, axis=-1)
        out = jnp.zeros_like(xf)
        for e in range(Wd.shape[0]):
            y = H @ Wd[e] + bd[e]
            sel = (assign == e)[:, None]
            out = out + jnp.where(sel, probs[:, e:e + 1] * y, 0.0)
        return out.reshape(orig_shape)

    def _L2_attn_ref(x, Wqkv, bqkv, W0, b0):
        import jax, jax.numpy as jnp
        import numpy as np
        B, N, D, H = (4, 256, 64, 8)
        b, n, d = x.shape
        h = Wqkv.shape[1] // (3 * d)
        qkv = x @ Wqkv + bqkv
        q, k, v = jnp.reshape(qkv, (3, b, n, d, h))
        score = jnp.einsum('bnqh,btqh->bnth', q, k) * d ** (-0.5)
        attn = jax.nn.softmax(score, axis=1)
        av = jnp.einsum('bnnh,bnqh->bnqh', attn, v)
        out = av.reshape(b, n, d * h) @ W0 + b0
        return out

    def _L2_ffn_ref(x, Wq_pk, pk_keys, Wq, keys_table, values_table, Wo):
        import jax, jax.numpy as jnp
        import numpy as np
        DIM = 64
        HEADS = 8
        NUM_KEYS = 64
        NUM_KV = NUM_KEYS ** 2
        PK_TOPK = 16
        FINAL_TOPK = 16
        DIM_KEY = DIM // 2
        P = 2

        def _pk(x, Wq_pk, pk_keys):
            b, n, _ = x.shape
            q = (x @ Wq_pk).reshape(b, n, P, HEADS, DIM_KEY).transpose(2, 0, 1, 3, 4)
            sim = jnp.einsum('pbnhd,pkhd->pbnhk', q, pk_keys)
            scores, idx = jax.lax.top_k(sim, PK_TOPK)
            idx0 = idx[0]
            idx1 = idx[1] * NUM_KEYS
            index = (idx0[..., :, None] + idx1[..., None, :]).reshape(b, n, HEADS, PK_TOPK * PK_TOPK)
            score = (scores[0][..., :, None] + scores[1][..., None, :]).reshape(b, n, HEADS, PK_TOPK * PK_TOPK)
            final_scores, pk_idx = jax.lax.top_k(score, FINAL_TOPK)
            final_indices = jnp.take_along_axis(index, pk_idx, axis=-1)
            final_scores = jax.nn.softmax(final_scores, axis=-1)
            return (final_scores, final_indices)
        b, n, d = x.shape
        q = (x @ Wq).reshape(b, n, HEADS, DIM) * DIM ** (-0.5)
        kv_scores, indices = _pk(x, Wq_pk, pk_keys)
        offsets = jnp.arange(HEADS, dtype=indices.dtype) * NUM_KV
        ind = indices + offsets[None, None, :, None]
        k = jnp.einsum('bnhk,bnhkd->bnhd', kv_scores, keys_table[ind])
        v = jnp.einsum('bnhk,bnhkd->bnhd', kv_scores, values_table[ind])
        sim = jnp.einsum('bihd,bjhd->bhij', q, k)
        neg = -jnp.finfo(sim.dtype).max
        causal = jnp.tril(jnp.ones((n, n), dtype=bool))
        sim = jnp.where(causal, sim, neg)
        attn = jax.nn.softmax(sim, axis=-1)
        out = jnp.einsum('bhij,bjhd->bhid', attn, v)
        out = out.transpose(0, 2, 1, 3).reshape(b, n, HEADS * DIM)
        return out @ Wo

    def _L3_attn_ref(node_features, ln_gamma, ln_beta, W_qkv, W_gate, b_gate, W_final, b_final):
        import jax, jax.numpy as jnp
        import numpy as np
        H, D = (8, 32)
        EPS = 1e-05
        x = node_features
        B, N, _ = x.shape
        mu = jnp.mean(x, axis=-1, keepdims=True)
        var = jnp.mean(jnp.square(x - mu), axis=-1, keepdims=True)
        normed = (x - mu) / jnp.sqrt(var + EPS) * ln_gamma + ln_beta
        qkv = normed @ W_qkv.T
        q, k, v = jnp.split(qkv, 3, axis=-1)

        def to_heads(t):
            return t.reshape(B, N, H, D).transpose(0, 2, 1, 3)
        q, k, v = (to_heads(q), to_heads(k), to_heads(v))
        gate = jax.nn.sigmoid(to_heads(x @ W_gate.T + b_gate))
        scores = jnp.einsum('bhid,bhjd->bhij', q, k) * D ** (-0.5)
        attn = jax.nn.softmax(scores, axis=-1)
        out = jnp.einsum('bhij,bhid->bhjd', attn, v) * gate
        out = out.transpose(0, 2, 1, 3).reshape(B, N, H * D)
        return x + out @ W_final.T + b_final

    def _L3_ffn_ref(x, W_gat, att_src, att_dst, b_gat, ln_gamma, ln_beta, W1, b1, W2, b2, edge_index):
        import jax, jax.numpy as jnp
        import numpy as np
        B, N, D = (16, 1024, 64)
        NUM_EXPERTS, TOP_K, HEADS = (4, 2, 4)
        N_EDGES = 262144
        LN_EPS = 1e-05

        def _layernorm(x, g, b):
            mu = x.mean(-1, keepdims=True)
            var = ((x - mu) ** 2).mean(-1, keepdims=True)
            return (x - mu) * jax.lax.rsqrt(var + LN_EPS) * g + b

        def _forward(x, edge_index, W_gat, att_src, att_dst, b_gat, ln_gamma, ln_beta, W1, b1, W2, b2):
            Bc, Nc, Dc = x.shape
            M = Bc * Nc
            x_flat = x.reshape(M, Dc)
            h = (x_flat @ W_gat).reshape(M, HEADS, NUM_EXPERTS)
            loops = jnp.arange(M, dtype=edge_index.dtype)
            src = jnp.concatenate([edge_index[0], loops])
            dst = jnp.concatenate([edge_index[1], loops])
            a_src = (h * att_src).sum(-1)
            a_dst = (h * att_dst).sum(-1)
            e = jax.nn.leaky_relu(a_src[src] + a_dst[dst], negative_slope=0.2)
            e_max = jax.ops.segment_max(e, dst, num_segments=M)
            ee = jnp.exp(e - e_max[dst])
            denom = jax.ops.segment_sum(ee, dst, num_segments=M)
            alpha = ee / (denom[dst] + 1e-16)
            msg = h[src] * alpha[:, :, None]
            agg = jax.ops.segment_sum(msg, dst, num_segments=M).reshape(M, HEADS * NUM_EXPERTS) + b_gat
            scores = _layernorm(agg, ln_gamma, ln_beta).reshape(M, HEADS, NUM_EXPERTS).mean(1)
            scores = scores.reshape(Bc, Nc, NUM_EXPERTS)
            topk_s, topk_i = jax.lax.top_k(scores, TOP_K)
            w = jax.nn.softmax(topk_s, axis=-1)
            out = jnp.zeros_like(x)
            for ei in range(NUM_EXPERTS):
                g = jnp.where(topk_i == ei, w, 0.0).sum(-1)
                hh = jax.nn.gelu(x @ W1[ei] + b1[ei], approximate=False)
                out = out + g[..., None] * (hh @ W2[ei] + b2[ei])
            return out
        return _forward(x, edge_index, W_gat, att_src, att_dst, b_gat, ln_gamma, ln_beta, W1, b1, W2, b2)
    h = _L0_tok_ref(x, L0_tok_W_qry, L0_tok_W_key, L0_tok_v, L0_tok_b)
    h = h + _L0_attn_ref(_layernorm(h, axis=-1), L0_attn_Wq, L0_attn_bq, L0_attn_Wk, L0_attn_bk, L0_attn_Wv, L0_attn_bv, L0_attn_Wu, L0_attn_bu)
    h = h + _L0_ffn_ref(_layernorm(h, axis=-1), L0_ffn_attention_mask, L0_ffn_wr, L0_ffn_br, L0_ffn_w1, L0_ffn_b1, L0_ffn_w2, L0_ffn_b2)
    h = h + _L1_attn_ref(_layernorm(h, axis=-1), L1_attn_wq, L1_attn_wkv, L1_attn_wo, L1_attn_q_norm_w, L1_attn_k_norm_w)
    h = h + _L1_ffn_ref(_layernorm(h, axis=-1), L1_ffn_W1, L1_ffn_b1, L1_ffn_Wg, L1_ffn_bg, L1_ffn_Wd, L1_ffn_bd)
    h = h + _L2_attn_ref(_layernorm(h, axis=-1), L2_attn_Wqkv, L2_attn_bqkv, L2_attn_W0, L2_attn_b0)
    h = h + _L2_ffn_ref(_layernorm(h, axis=-1), L2_ffn_Wq_pk, L2_ffn_pk_keys, L2_ffn_Wq, L2_ffn_keys_table, L2_ffn_values_table, L2_ffn_Wo)
    h = h + _L3_attn_ref(_layernorm(h, axis=-1), L3_attn_ln_gamma, L3_attn_ln_beta, L3_attn_W_qkv, L3_attn_W_gate, L3_attn_b_gate, L3_attn_W_final, L3_attn_b_final)
    h = h + _L3_ffn_ref(_layernorm(h, axis=-1), L3_ffn_W_gat, L3_ffn_att_src, L3_ffn_att_dst, L3_ffn_b_gat, L3_ffn_ln_gamma, L3_ffn_ln_beta, L3_ffn_W1, L3_ffn_b1, L3_ffn_W2, L3_ffn_b2, L3_ffn_edge_index)
    return h

_drawn_inputs = setup_inputs


def setup_inputs(seed=0):
    import zlib

    import numpy as np

    out = dict(_drawn_inputs(seed))
    spreads = {'L0_tok_b': (0.0, 0.8),
     'L0_attn_bq': (0.0, 0.8),
     'L0_attn_bk': (0.0, 2.0),
     'L0_attn_bv': (0.0, 0.1),
     'L0_attn_bu': (0.0, 0.1),
     'L0_ffn_b1': (0.0, 0.8),
     'L0_ffn_b2': (0.0, 0.8),
     'L1_attn_q_norm_w': (1.0, 0.6),
     'L1_attn_k_norm_w': (1.0, 0.6),
     'L1_ffn_b1': (0.0, 0.8),
     'L1_ffn_bg': (0.0, 0.581),
     'L1_ffn_bd': (0.0, 0.75),
     'L2_attn_bqkv': (0.0, 2.0),
     'L2_attn_b0': (0.0, 0.1),
     'L3_attn_ln_gamma': (1.0, 0.6),
     'L3_attn_ln_beta': (0.0, 0.8),
     'L3_attn_b_gate': (1.0, 0.6),
     'L3_attn_b_final': (0.0, 0.666),
     'L3_ffn_b_gat': (0.0, 1.762),
     'L3_ffn_ln_gamma': (1.0, 0.6),
     'L3_ffn_ln_beta': (0.0, 2.0),
     'L3_ffn_b1': (0.0, 2.0),
     'L3_ffn_b2': (0.0, 0.694)}
    factors = {'L0_attn_Wq': 8.0,
     'L0_attn_Wk': 8.0,
     'L0_ffn_wr': 6.557,
     'L0_ffn_w1': 8.0,
     'L0_ffn_w2': 8.0,
     'L1_attn_wq': 3.206,
     'L1_ffn_W1': 7.384,
     'L1_ffn_Wg': 7.906,
     'L1_ffn_Wd': 8.0,
     'L2_attn_Wqkv': 64.0,
     'L2_attn_W0': 64.0,
     'L2_ffn_Wq_pk': 8.0,
     'L2_ffn_pk_keys': 8.0,
     'L2_ffn_Wq': 64.0,
     'L2_ffn_keys_table': 64.0,
     'L2_ffn_values_table': 8.0,
     'L2_ffn_Wo': 8.0,
     'L3_attn_W_qkv': 7.563,
     'L3_attn_W_gate': 8.0,
     'L3_attn_W_final': 7.458,
     'L3_ffn_att_src': 64.0,
     'L3_ffn_att_dst': 200.0,
     'L3_ffn_W_gat': 7.088,
     'L3_ffn_W1': 3.862}
    for name, (base, spread) in spreads.items():
        noise = np.random.default_rng([zlib.crc32(name.encode()), seed]).standard_normal(out[name].shape)
        drawn = base * np.exp(spread * noise) if base else spread * noise
        out[name] = jnp.asarray(drawn.astype(out[name].dtype))
    for name, factor in factors.items():
        out[name] = (out[name] * factor).astype(out[name].dtype)
    return out
```

```python
from contextlib import ExitStack

import numpy as np
import concourse.bass as bass
from concourse import mybir

F32 = mybir.dt.float32
BF16 = mybir.dt.bfloat16
F16 = mybir.dt.float16
I32 = mybir.dt.int32
U32 = mybir.dt.uint32
ALU = mybir.AluOpType
ACT = mybir.ActivationFunctionType
AX = mybir.AxisListType

B, L, C = 32, 250, 64
WIN = 9
T = L - WIN + 1
NT = 2
TP = T // NT
TILES = B * NT
M = B * T
NEG = -1e30
LANES = 2
PAIRS = B // LANES
BANK = 512


class Chain:

    def __init__(self, sems, phases):
        self.sem = sems
        self.end, total = {}, 1
        for p in phases:
            name, _, weight = p.partition(":")
            assert name not in self.end, name
            total += int(weight or 1)
            self.end[name] = total
        self.per = total - 1

    def after(self, i, name):
        return i * self.per + self.end[name]

    def before(self, i):
        return i * self.per + 1


def row(ap):
    return ap.rearrange("(a n) -> a n", a=1)


def spread(ap, k):
    return ap.unsqueeze(len(ap.shape)).to_broadcast(list(ap.shape) + [k])


def repeat(ap, k):
    return ap.unsqueeze(1).to_broadcast([ap.shape[0], k] + list(ap.shape[1:]))


def load_all(nc, ctx, name, pairs, ones=()):
    sem = ctx.enter_context(nc.semaphore(name + "_loaded"))
    pre = ctx.enter_context(nc.semaphore(name + "_preset"))
    with nc.Block() as block:
        @block.vector
        def _(v):
            for ap, value in ones:
                v.memset(ap, value).then_inc(pre, 1)

        @block.sync
        def _(sp):
            if ones:
                sp.wait_ge(pre, len(ones))
            for dst, src in pairs:
                sp.dma_start(dst, src).then_inc(sem, 16)
            sp.wait_ge(sem, 16 * len(pairs))


def layernorm_all(nc, h, xn, name):
    with ExitStack() as ctx:
        sq = ctx.enter_context(nc.sbuf_tensor(name + "_sq", [TP, TILES, C], F32))
        st = ctx.enter_context(nc.sbuf_tensor(name + "_st", [TP, 4, TILES], F32))
        done = ctx.enter_context(nc.semaphore(name + "_ln_dve_step"))
        root = ctx.enter_context(nc.semaphore(name + "_ln_std_ready"))
        mean, var, std, rstd = (st[:, k, :] for k in range(4))
        with nc.Block() as block:
            @block.vector
            def _(v):
                v.tensor_reduce(mean, h[:, :, :], AX.X, ALU.add).then_inc(done, 1)
                v.wait_ge(done, 1)
                v.tensor_scalar(mean, mean, 1.0 / C, None, ALU.mult).then_inc(done, 1)
                v.wait_ge(done, 2)
                v.tensor_tensor(xn[:, :, :], h[:, :, :], spread(mean, C), ALU.subtract).then_inc(done, 1)
                v.wait_ge(done, 3)
                v.tensor_tensor(sq[:, :, :], xn[:, :, :], xn[:, :, :], ALU.mult).then_inc(done, 1)
                v.wait_ge(done, 4)
                v.tensor_reduce(var, sq[:, :, :], AX.X, ALU.add).then_inc(done, 1)
                v.wait_ge(done, 5)
                v.tensor_scalar(var, var, 1.0 / C, 1e-5, ALU.mult, ALU.add).then_inc(done, 1)
                v.wait_ge(root, 1)
                v.reciprocal(rstd, std).then_inc(done, 1)
                v.wait_ge(done, 7)
                v.tensor_tensor(xn[:, :, :], xn[:, :, :], spread(rstd, C), ALU.mult).then_inc(done, 1)

            @block.scalar
            def _(a):
                a.wait_ge(done, 6)
                a.activation(std, var, ACT.Sqrt).then_inc(root, 1)


def start_lanes(sp, chain):
    for s in chain.sem:
        sp.sem_inc(s, 1)


def stage_tok(nc, h, k, A):
    W0 = WIN // 2
    with ExitStack() as ctx:
        sb = lambda n, s, d=F32: ctx.enter_context(nc.sbuf_tensor("tok_" + n, s, d))
        wkey, wqry, vblk = sb("wkey", [128, 128]), sb("wqry", [128, 128]), sb("vblk", [128, 128])
        bias, vcol = sb("bias", [128, 1]), sb("vcol", [128, 1])
        x = sb("x", [128, L])
        key, qry = sb("key", [128, L]), sb("qry", [128, T])
        th, e = sb("th", [128, WIN, T]), sb("e", [128, WIN, T])
        mx, den, num = sb("mx", [128, T]), sb("den", [128, T]), sb("num", [128, T])
        ps = ctx.enter_context(nc.psum_tensor("tok_ps", [128, 8, BANK], F32))
        pairs = [(bias[k2 * C:(k2 + 1) * C, :], A["L0_tok_b"].rearrange("(n a) -> n a", a=1)) for k2 in range(2)]
        for k2 in range(2):
            s = slice(k2 * C, (k2 + 1) * C)
            pairs += [(wkey[s, s], A["L0_tok_W_key"]), (wqry[s, s], A["L0_tok_W_qry"]),
                      (vcol[s, :], A["L0_tok_v"].rearrange("(n a) -> n a", a=1))]
        load_all(nc, ctx, "tok", pairs, [(wkey[:, :], 0.0), (wqry[:, :], 0.0), (vblk[:, :], 0.0)])
        with nc.Block() as block:
            @block.vector
            def _(v):
                for k2 in range(2):
                    s = slice(k2 * C, (k2 + 1) * C)
                    v.tensor_scalar(vblk[s, s], wkey[s, s], 0.0, vcol[s, :], ALU.mult, ALU.add)
        ch = Chain([ctx.enter_context(nc.semaphore("tok_step"))], [
            "x:16", "project", "evac", "add", "tanh", "score", "score_out", "max", "sub", "exp",
            "den", "weigh", "num", "recip", "out", "turn", "store"])
        step = ch.sem[0]
        TPS = [(s, ps[:, s // 2, (s % 2) * T:(s % 2 + 1) * T]) for s in range(WIN)]
        with nc.Block() as block:
            @block.sync
            def _(sp):
                sp.sem_inc(step, 1)
                with sp.Fori(0, B // 2) as i:
                    sp.wait_ge(step, ch.before(i))
                    sp.dma_start(x[:, :], A["xT"][bass.ds(i, 1), :, :].rearrange("a p n -> (a p) n")).then_inc(step, 16)

            @block.tensor
            def _(pe):
                with pe.Fori(0, B // 2) as i:
                    pe.wait_ge(step, ch.after(i, "x"))
                    pe.matmul(ps[:, 5, 0:L], wkey[:, :], x[:, :], start=True, stop=True)
                    pe.matmul(ps[:, 6, 0:T], wqry[:, :], x[:, W0:W0 + T], start=True, stop=True).then_inc(step, 1)
                    pe.wait_ge(step, ch.after(i, "tanh"))
                    for s, dst in TPS:
                        mm = pe.matmul(dst, vblk[:, :], th[:, s, :], start=True, stop=True)
                    mm.then_inc(step, 1)
                    pe.wait_ge(step, ch.after(i, "out"))
                    for t in range(NT):
                        mm = pe.transpose(ps[0:TP, 7, t * 128:(t + 1) * 128], num[:, t * TP:(t + 1) * TP], k["ident"][:, :])
                    mm.then_inc(step, 1)

            @block.scalar
            def _(a):
                with a.Fori(0, B // 2) as i:
                    a.wait_ge(step, ch.after(i, "project"))
                    a.activation(key[:, :], ps[:, 5, 0:L], ACT.Copy)
                    a.activation(qry[:, :], ps[:, 6, 0:T], ACT.Identity, bias=bias[:, :]).then_inc(step, 1)
                    a.wait_ge(step, ch.after(i, "add"))
                    a.activation(th[:, :, :], th[:, :, :], ACT.Tanh).then_inc(step, 1)
                    a.wait_ge(step, ch.after(i, "score"))
                    a.activation(e[:, 0:8, :].rearrange("p (k s) w -> p k (s w)", s=2), ps[:, 0:4, 0:2 * T], ACT.Copy)
                    a.activation(e[:, 8, :], ps[:, 4, 0:T], ACT.Copy).then_inc(step, 1)
                    a.wait_ge(step, ch.after(i, "sub"))
                    a.activation(e[:, :, :], e[:, :, :], ACT.Exp).then_inc(step, 1)

            @block.vector
            def _(v):
                with v.Fori(0, B // 2) as i:
                    v.wait_ge(step, ch.after(i, "evac"))
                    for s in range(WIN):
                        ins = v.tensor_tensor(th[:, s, :], key[:, s:s + T], qry[:, :], ALU.add)
                    ins.then_inc(step, 1)
                    v.wait_ge(step, ch.after(i, "score_out"))
                    v.tensor_reduce(mx[:, :], e[:, :, :].rearrange("p s w -> p w s"), AX.X, ALU.max).then_inc(step, 1)
                    v.wait_ge(step, ch.after(i, "max"))
                    v.tensor_tensor(e[:, :, :], e[:, :, :], repeat(mx[:, :], WIN), ALU.subtract).then_inc(step, 1)
                    v.wait_ge(step, ch.after(i, "exp"))
                    v.tensor_reduce(den[:, :], e[:, :, :].rearrange("p s w -> p w s"), AX.X, ALU.add).then_inc(step, 1)
                    v.wait_ge(step, ch.after(i, "den"))
                    for s in range(WIN):
                        ins = v.tensor_tensor(e[:, s, :], e[:, s, :], x[:, s:s + T], ALU.mult)
                    ins.then_inc(step, 1)
                    v.wait_ge(step, ch.after(i, "weigh"))
                    v.tensor_reduce(num[:, :], e[:, :, :].rearrange("p s w -> p w s"), AX.X, ALU.add).then_inc(step, 1)
                    v.wait_ge(step, ch.after(i, "num"))
                    v.reciprocal(den[:, :], den[:, :]).then_inc(step, 1)
                    v.wait_ge(step, ch.after(i, "recip"))
                    v.tensor_tensor(num[:, :], num[:, :], den[:, :], ALU.mult).then_inc(step, 1)
                    v.wait_ge(step, ch.after(i, "turn"))
                    v.tensor_copy(h[:, bass.ds(i * 4, 4), :].rearrange("p (b t) c -> p t b c", b=2),
                                  ps[0:TP, 7, 0:256].rearrange("p (t b c) -> p t b c", t=NT, b=2)).then_inc(step, 1)


def stage_l0_attn(nc, h, xn, k, A):
    NH, CA = 8, C + 1
    with ExitStack() as ctx:
        sb = lambda n, s, d=F32: ctx.enter_context(nc.sbuf_tensor("a0_" + n, s, d))
        wq, wk, wv = sb("wq", [C, NH, CA]), sb("wk", [C, NH, CA]), sb("wv", [C, NH, CA])
        wu, bu = sb("wu", [C, NH, C]), sb("bu", [TP, C])
        mask, valid = sb("mask", [TP, NT, T]), sb("valid", [TP, NT])
        mm_, vu = sb("m", [CA, NH, CA]), sb("vu", [CA, NH, C])
        xs = [sb(f"xs{c}", [TP, NT, C]) for c in range(LANES)]
        xT = [sb(f"xT{c}", [CA, T]) for c in range(LANES)]
        vs = [sb(f"vs{c}", [TP, NT, NH * C]) for c in range(LANES)]
        NS = 4
        subs = [(c, g) for g in range(NS) for c in range(LANES)]
        per = lambda n, shape: {cg: sb(f"{n}{cg[0]}{cg[1]}", shape) for cg in subs}
        y, s, pT = per("y", [CA, T]), per("s", [TP, NT, T]), per("pT", [TP, NT, T])
        nmax, den, acc = per("nmax", [TP, NT]), per("den", [TP, NT]), per("acc", [TP, NT, C])
        red = [sb(f"red{c}", [TP, NT, C]) for c in range(LANES)]
        ps = [ctx.enter_context(nc.psum_tensor(f"a0_ps{c}", [128, 4, BANK], F32)) for c in range(LANES)]
        folded = ctx.enter_context(nc.semaphore("a0_folded"))
        moved = ctx.enter_context(nc.semaphore("a0_fold_moved"))
        load_all(nc, ctx, "a0", [
            (wq[:, :, :], A["L0_attn_WqT"]), (wk[:, :, :], A["L0_attn_WkT"]), (wv[:, :, :], A["L0_attn_WvT"]),
            (wu[:, :, :], A["L0_attn_WuH"]), (bu[:, :], row(A["L0_attn_bu"]).to_broadcast([TP, C])),
            (mask[:, :, :], k["strict"]), (valid[:, :], k["valid"])],
            [(xT[c][C:CA, :], 1.0) for c in range(LANES)])
        ident = k["ident"]
        with nc.Block() as block:
            @block.tensor
            def _(pe):
                for n in range(NH):
                    pe.matmul(ps[0][0:CA, n % 4, 0:CA], wq[:, n, :], wk[:, n, :], start=True, stop=True)
                    pe.matmul(ps[1][0:CA, n % 4, 0:C], wv[:, n, :], wu[:, n, :], start=True, stop=True).then_inc(folded, 1)
                    pe.wait_ge(moved, n + 1)

            @block.scalar
            def _(a):
                for n in range(NH):
                    a.wait_ge(folded, n + 1)
                    a.activation(mm_[:, n, :], ps[0][0:CA, n % 4, 0:CA], ACT.Copy)
                    a.activation(vu[:, n, :], ps[1][0:CA, n % 4, 0:C], ACT.Copy).then_inc(moved, 1)

        ch = Chain([ctx.enter_context(nc.semaphore(f"a0_step{c}")) for c in range(LANES)],
                   ["x", "turn", "xT", "v", "v_out", "red0", "red1", "red2", "bias", "add"])
        hd = Chain([ctx.enter_context(nc.semaphore(f"a0_head{c}{g}")) for c, g in subs],
                   [f"{r}.{p}" for r in range(NH // NS) for p in
                    ("y", "y_out", "s", "mask", "max", "nmax", "exp", "turn", "pT", "pv", "recip", "valid", "acc")])
        step, done, both = ch.sem, ch.after, range(LANES)
        head, ready = dict(zip(subs, hd.sem)), hd.after
        with nc.Block() as block:
            @block.sync
            def _(sp):
                start_lanes(sp, ch)
                start_lanes(sp, hd)

            @block.tensor
            def _(pe):
                with pe.Fori(0, PAIRS) as i:
                    for c in both:
                        pe.wait_ge(step[c], done(i, "x"))
                        pe.transpose(ps[c][:, 0, 0:TP], xs[c][:, :, :].rearrange("p t c -> p (t c)"),
                                     ident[0:TP, 0:TP]).then_inc(step[c], 1)
                    for c in both:
                        pe.wait_ge(step[c], done(i, "xT"))
                        for t in range(NT):
                            ins = pe.matmul(ps[c][0:TP, 2 + t, :], xT[c][:, t * TP:(t + 1) * TP],
                                            vu[:, :, :].rearrange("p n c -> p (n c)"), start=True, stop=True)
                        ins.then_inc(step[c], 1)
                    for r in range(NH // NS):
                        for c, g in subs:
                            n = NS * r + g
                            if r == 0:
                                pe.wait_ge(step[c], done(i, "v_out"))
                            else:
                                pe.wait_ge(head[c, g], ready(i, f"{r - 1}.acc"))
                            pe.matmul(ps[c][0:CA, g, 0:T], mm_[:, n, :], xT[c][:, :], start=True, stop=True).then_inc(head[c, g], 1)
                        for c, g in subs:
                            pe.wait_ge(head[c, g], ready(i, f"{r}.y_out"))
                            for t in range(NT):
                                ins = pe.matmul(ps[c][0:TP, g, t * T:(t + 1) * T], y[c, g][:, t * TP:(t + 1) * TP], xT[c][:, :],
                                                start=True, stop=True)
                            ins.then_inc(head[c, g], 1)
                        for c, g in subs:
                            pe.wait_ge(head[c, g], ready(i, f"{r}.exp"))
                            for j in range(NT):
                                for t in range(NT):
                                    ins = pe.transpose(ps[c][0:TP, g, j * T + t * TP:j * T + (t + 1) * TP],
                                                       s[c, g][:, t, j * TP:(j + 1) * TP], ident[0:TP, 0:TP])
                            ins.then_inc(head[c, g], 1)
                        for c, g in subs:
                            n = NS * r + g
                            pe.wait_ge(head[c, g], ready(i, f"{r}.pT"))
                            for t in range(NT):
                                for j in range(NT):
                                    ins = pe.matmul(ps[c][0:TP, g, t * C:(t + 1) * C], pT[c, g][:, j, t * TP:(t + 1) * TP],
                                                    vs[c][:, j, n * C:(n + 1) * C], start=(j == 0), stop=(j == NT - 1))
                            ins.then_inc(head[c, g], 1)

            @block.scalar
            def _(a):
                with a.Fori(0, PAIRS) as i:
                    for c in both:
                        a.wait_ge(step[c], done(i, "turn"))
                        for t in range(NT):
                            ins = a.activation(xT[c][0:C, t * TP:(t + 1) * TP], ps[c][t * C:(t + 1) * C, 0, 0:TP], ACT.Copy)
                        ins.then_inc(step[c], 1)
                    for c in both:
                        a.wait_ge(step[c], done(i, "v"))
                        a.activation(vs[c][:, :, :], ps[c][0:TP, 2:4, :], ACT.Copy).then_inc(step[c], 1)
                    for r in range(NH // NS):
                        for c, g in subs:
                            a.wait_ge(head[c, g], ready(i, f"{r}.y"))
                            a.activation(y[c, g][:, :], ps[c][0:CA, g, 0:T], ACT.Copy).then_inc(head[c, g], 1)
                        for c, g in subs:
                            a.wait_ge(head[c, g], ready(i, f"{r}.nmax"))
                            for t in range(NT):
                                ins = a.activation(s[c, g][:, t, :], s[c, g][:, t, :], ACT.Exp, bias=nmax[c, g][:, t:t + 1],
                                                   scale=C ** -0.5, accum_out=den[c, g][:, t:t + 1])
                            ins.then_inc(head[c, g], 1)
                        for c, g in subs:
                            a.wait_ge(head[c, g], ready(i, f"{r}.turn"))
                            a.activation(pT[c, g][:, :, :].rearrange("p j w -> p (j w)"), ps[c][0:TP, g, 0:NT * T],
                                         ACT.Copy).then_inc(head[c, g], 1)

            @block.vector
            def _(v):
                with v.Fori(0, PAIRS) as i:
                    tiles = [bass.ds(i * (LANES * NT) + c * NT, NT) for c in both]
                    for c in both:
                        v.wait_ge(step[c], ch.before(i))
                        v.tensor_copy(xs[c][:, :, :], xn[:, tiles[c], :]).then_inc(step[c], 1)
                    for r in range(NH // NS):
                        for c, g in subs:
                            v.wait_ge(head[c, g], ready(i, f"{r}.s"))
                            v.tensor_tensor(s[c, g][:, :, :].rearrange("p t w -> p (t w)"), ps[c][0:TP, g, 0:NT * T],
                                            mask[:, :, :].rearrange("p t w -> p (t w)"), ALU.add).then_inc(head[c, g], 1)
                            v.wait_ge(head[c, g], ready(i, f"{r}.mask"))
                            v.tensor_reduce(nmax[c, g][:, :], s[c, g][:, :, :], AX.X, ALU.max).then_inc(head[c, g], 1)
                            v.wait_ge(head[c, g], ready(i, f"{r}.max"))
                            v.tensor_scalar(nmax[c, g][:, :], nmax[c, g][:, :], -C ** -0.5, None, ALU.mult).then_inc(head[c, g], 1)
                        for c, g in subs:
                            v.wait_ge(head[c, g], ready(i, f"{r}.pv"))
                            v.reciprocal(den[c, g][:, :], den[c, g][:, :]).then_inc(head[c, g], 1)
                        for c, g in subs:
                            v.wait_ge(head[c, g], ready(i, f"{r}.recip"))
                            v.tensor_tensor(den[c, g][:, :], den[c, g][:, :], valid[:, :], ALU.mult).then_inc(head[c, g], 1)
                        for c, g in subs:
                            v.wait_ge(head[c, g], ready(i, f"{r}.valid"))
                            for t in range(NT):
                                out = ps[c][0:TP, g, t * C:(t + 1) * C]
                                if r == 0:
                                    ins = v.tensor_scalar(acc[c, g][:, t, :], out, den[c, g][:, t:t + 1], None, ALU.mult)
                                else:
                                    ins = v.scalar_tensor_tensor(out=acc[c, g][:, t, :], in0=out, scalar=den[c, g][:, t:t + 1],
                                                                 in1=acc[c, g][:, t, :], op0=ALU.mult, op1=ALU.add)
                            ins.then_inc(head[c, g], 1)
                    for c in both:
                        v.wait_ge(step[c], done(i, "v_out"))
                        for g in range(NS):
                            v.wait_ge(head[c, g], ready(i, f"{NH // NS - 1}.acc"))
                        v.tensor_tensor(red[c][:, :, :], acc[c, 0][:, :, :], acc[c, 1][:, :, :], ALU.add).then_inc(step[c], 1)
                    for c in both:
                        v.wait_ge(step[c], done(i, "red0"))
                        v.tensor_tensor(red[c][:, :, :], red[c][:, :, :], acc[c, 2][:, :, :], ALU.add).then_inc(step[c], 1)
                    for c in both:
                        v.wait_ge(step[c], done(i, "red1"))
                        v.tensor_tensor(red[c][:, :, :], red[c][:, :, :], acc[c, 3][:, :, :], ALU.add).then_inc(step[c], 1)
                    for c in both:
                        v.wait_ge(step[c], done(i, "red2"))
                        v.tensor_tensor(red[c][:, :, :], red[c][:, :, :], repeat(bu[:, :], NT), ALU.add).then_inc(step[c], 1)
                    for c in both:
                        v.wait_ge(step[c], done(i, "bias"))
                        v.tensor_tensor(h[:, tiles[c], :], h[:, tiles[c], :], red[c][:, :, :], ALU.add).then_inc(step[c], 1)


def stage_l0_ffn(nc, h, xn, k, A):
    CA, H = C + 1, 256
    KK = T // 2 - 1
    NC = H // 128
    with ExitStack() as ctx:
        sb = lambda n, s, d=F32: ctx.enter_context(nc.sbuf_tensor("f0_" + n, s, d))
        w1, wr = sb("w1", [CA, H]), sb("wr", [CA, 1])
        w2, b2 = sb("w2", [128, NC, C]), sb("b2", [TP, C])
        own, before, ones = sb("own", [TP, NT, T]), sb("before", [TP, NT, T]), sb("ones", [TP, 128])
        xs = [sb(f"xs{c}", [TP, NT, C]) for c in range(LANES)]
        xT = [sb(f"xT{c}", [CA, T]) for c in range(LANES)]
        w = [sb(f"wt{c}", [TP, NT]) for c in range(LANES)]
        dg = [sb(f"dg{c}", [TP, NT, T]) for c in range(LANES)]
        gt = [sb(f"gt{c}", [TP, NT, T]) for c in range(LANES)]
        eq = [sb(f"eq{c}", [TP, NT, T]) for c in range(LANES)]
        rank = [sb(f"rank{c}", [TP, NT]) for c in range(LANES)]
        hid = [sb(f"hid{c}", [128, NC, T]) for c in range(LANES)]
        y = [sb(f"y{c}", [TP, NT, C]) for c in range(LANES)]
        ps = [ctx.enter_context(nc.psum_tensor(f"f0_ps{c}", [128, 4, BANK], F32)) for c in range(LANES)]
        load_all(nc, ctx, "f0", [
            (w1[0:C, :], A["L0_ffn_w1"]), (w1[C:CA, :], row(A["L0_ffn_b1"])),
            (wr[0:C, :], A["L0_ffn_wr"]), (wr[C:CA, :], row(A["L0_ffn_br"])),
            (w2[:, :, :], A["L0_ffn_w2"].rearrange("(n p) c -> p n c", p=128)),
            (b2[:, :], row(A["L0_ffn_b2"]).to_broadcast([TP, C])),
            (own[:, :, :], k["own"]), (before[:, :, :], k["before"])],
            [(xT[c][C:CA, :], 1.0) for c in range(LANES)] + [(ones[:, :], 1.0)])
        ch = Chain([ctx.enter_context(nc.semaphore(f"f0_step{c}")) for c in range(LANES)], [
            "x", "turn", "xT", "route", "w", "diag", "spread", "compare", "ties", "count", "rank", "sel", "scale",
            "hid", "gelu", "y", "b2", "gate", "res", "add"])
        step, done, both = ch.sem, ch.after, range(LANES)
        with nc.Block() as block:
            @block.sync
            def _(sp):
                start_lanes(sp, ch)

            @block.tensor
            def _(pe):
                with pe.Fori(0, PAIRS) as i:
                    for c in both:
                        pe.wait_ge(step[c], done(i, "x"))
                        pe.transpose(ps[c][:, 0, 0:TP], xs[c][:, :, :].rearrange("p t c -> p (t c)"),
                                     k["ident"][0:TP, 0:TP]).then_inc(step[c], 1)
                    for c in both:
                        pe.wait_ge(step[c], done(i, "xT"))
                        for t in range(NT):
                            ins = pe.matmul(ps[c][0:TP, 1, t:t + 1], xT[c][:, t * TP:(t + 1) * TP], wr[:, :], start=True, stop=True)
                        ins.then_inc(step[c], 1)
                    for c in both:
                        pe.wait_ge(step[c], done(i, "diag"))
                        for t in range(NT):
                            ins = pe.matmul(ps[c][:, 2, 0:T], ones[:, :], dg[c][:, t, :], start=(t == 0), stop=(t == NT - 1))
                        ins.then_inc(step[c], 1)
                    for c in both:
                        pe.wait_ge(step[c], done(i, "scale"))
                        for n in range(NC):
                            ins = pe.matmul(ps[c][:, 3, n * T:(n + 1) * T], w1[:, n * 128:(n + 1) * 128], xT[c][:, :],
                                            start=True, stop=True)
                        ins.then_inc(step[c], 1)
                    for c in both:
                        pe.wait_ge(step[c], done(i, "gelu"))
                        for t in range(NT):
                            for n in range(NC):
                                ins = pe.matmul(ps[c][0:TP, 0, t * C:(t + 1) * C], hid[c][:, n, t * TP:(t + 1) * TP], w2[:, n, :],
                                                start=(n == 0), stop=(n == NC - 1))
                        ins.then_inc(step[c], 1)

            @block.scalar
            def _(a):
                with a.Fori(0, PAIRS) as i:
                    for c in both:
                        a.wait_ge(step[c], done(i, "turn"))
                        for t in range(NT):
                            ins = a.activation(xT[c][0:C, t * TP:(t + 1) * TP], ps[c][t * C:(t + 1) * C, 0, 0:TP], ACT.Copy)
                        ins.then_inc(step[c], 1)
                    for c in both:
                        a.wait_ge(step[c], done(i, "hid"))
                        a.activation(hid[c][:, :, :].rearrange("p n w -> p (n w)"), ps[c][:, 3, 0:NC * T],
                                     ACT.Gelu_apprx_tanh).then_inc(step[c], 1)

            @block.vector
            def _(v):
                flat = lambda ap: ap[:, :, :].rearrange("p t w -> p (t w)")
                with v.Fori(0, PAIRS) as i:
                    tiles = [bass.ds(i * (LANES * NT) + c * NT, NT) for c in both]
                    for c in both:
                        v.wait_ge(step[c], ch.before(i))
                        v.tensor_copy(xs[c][:, :, :], xn[:, tiles[c], :]).then_inc(step[c], 1)
                    for c in both:
                        v.wait_ge(step[c], done(i, "route"))
                        v.tensor_copy(w[c][:, :], ps[c][0:TP, 1, 0:NT]).then_inc(step[c], 1)
                    for c in both:
                        v.wait_ge(step[c], done(i, "w"))
                        v.tensor_tensor(dg[c][:, :, :], own[:, :, :], spread(w[c][:, :], T), ALU.mult).then_inc(step[c], 1)
                    for c in both:
                        v.wait_ge(step[c], done(i, "spread"))
                        row_w = repeat(ps[c][0:TP, 2, 0:T], NT)
                        v.tensor_tensor(gt[c][:, :, :], row_w, spread(w[c][:, :], T), ALU.is_gt)
                        v.tensor_tensor(eq[c][:, :, :], row_w, spread(w[c][:, :], T), ALU.is_equal).then_inc(step[c], 1)
                    for c in both:
                        v.wait_ge(step[c], done(i, "compare"))
                        v.tensor_tensor(flat(eq[c]), flat(eq[c]), flat(before), ALU.mult).then_inc(step[c], 1)
                    for c in both:
                        v.wait_ge(step[c], done(i, "ties"))
                        v.tensor_tensor(flat(gt[c]), flat(gt[c]), flat(eq[c]), ALU.add).then_inc(step[c], 1)
                    for c in both:
                        v.wait_ge(step[c], done(i, "count"))
                        v.tensor_reduce(rank[c][:, :], gt[c][:, :, :], AX.X, ALU.add).then_inc(step[c], 1)
                    for c in both:
                        v.wait_ge(step[c], done(i, "rank"))
                        v.tensor_scalar(rank[c][:, :], rank[c][:, :], float(KK), None, ALU.is_lt).then_inc(step[c], 1)
                    for c in both:
                        v.wait_ge(step[c], done(i, "sel"))
                        v.tensor_tensor(rank[c][:, :], rank[c][:, :], w[c][:, :], ALU.mult).then_inc(step[c], 1)
                    for c in both:
                        v.wait_ge(step[c], done(i, "y"))
                        v.tensor_tensor(y[c][:, :, :], ps[c][0:TP, 0, 0:NT * C].rearrange("p (t c) -> p t c", t=NT),
                                        repeat(b2[:, :], NT), ALU.add).then_inc(step[c], 1)
                    for c in both:
                        v.wait_ge(step[c], done(i, "b2"))
                        v.tensor_tensor(y[c][:, :, :], y[c][:, :, :], spread(rank[c][:, :], C), ALU.mult).then_inc(step[c], 1)
                    for c in both:
                        v.wait_ge(step[c], done(i, "gate"))
                        v.tensor_tensor(y[c][:, :, :], y[c][:, :, :], xs[c][:, :, :], ALU.add).then_inc(step[c], 1)
                    for c in both:
                        v.wait_ge(step[c], done(i, "res"))
                        v.tensor_tensor(h[:, tiles[c], :], h[:, tiles[c], :], y[c][:, :, :], ALU.add).then_inc(step[c], 1)


def stage_l1_attn(nc, h, xn, k, A):
    NH, NS = 16, 4
    EPS = 1.1920929e-07
    with ExitStack() as ctx:
        sb = lambda n, s, d=F32: ctx.enter_context(nc.sbuf_tensor("a1_" + n, s, d))
        wq2, wq = sb("wq2", [C, NH, 2 * C]), sb("wq", [C, NH * C])
        wkv, wv, wo, vo = sb("wkv", [C, 2 * C]), sb("wv", [C, C]), sb("wo", [C, NH * C]), sb("vo", [C, NH * C])
        rope, fold, wn, wn2 = sb("rope", [128, T]), sb("fold", [128, 128]), sb("wn", [128, 1]), sb("wn2", [128, 1])
        mask = sb("mask", [TP, NT, T])
        eps = sb("eps", [TP, 1])
        both = range(LANES)
        xs = [sb(f"xs{c}", [TP, NT, C]) for c in both]
        xT = [sb(f"xT{c}", [C, T]) for c in both]
        vs = [sb(f"vs{c}", [TP, NT, NH * C]) for c in both]
        sq = vs
        rms = [sb(f"rms{c}", [TP, NT, NH + 1]) for c in both]
        ks = [sb(f"ks{c}", [TP, NT, 2 * C]) for c in both]
        kr = [sb(f"kr{c}", [128, T]) for c in both]
        kd = [sb(f"kd{c}", [128, T]) for c in both]
        subs = [(c, g) for g in range(NS) for c in both]
        per = lambda n, shape: {cg: sb(f"{n}{cg[0]}{cg[1]}", shape) for cg in subs}
        y, s, pT = per("y", [128, T]), per("s", [TP, NT, T]), per("pT", [TP, NT, T])
        nmax, den, acc = per("nmax", [TP, NT]), per("den", [TP, NT]), per("acc", [TP, NT, C])
        red = [sb(f"red{c}", [TP, NT, C]) for c in both]
        ps = [ctx.enter_context(nc.psum_tensor(f"a1_ps{c}", [128, 4, BANK], F32)) for c in both]
        folded = ctx.enter_context(nc.semaphore("a1_folded"))
        moved = ctx.enter_context(nc.semaphore("a1_fold_moved"))
        col = lambda ap: ap.rearrange("(n a) -> n a", a=1)
        load_all(nc, ctx, "a1", [
            (wq2[:, :, :], A["L1_attn_wq2"]), (wq[:, :], A["L1_attn_wqT"]), (wkv[:, :], A["L1_attn_wk2"]),
            (wv[:, :], A["L1_attn_wkv"][C:2 * C, :]), (wo[:, :], A["L1_attn_woH"]),
            (rope[:, :], k["rope"]), (fold[:, :], k["fold"]), (mask[:, :, :], k["window"])] + [
            (w[q * C:(q + 1) * C, :], col(A[f"L1_attn_{n}_norm_w"])) for w, n in ((wn, "q"), (wn2, "k")) for q in range(2)],
            [(eps[:, :], EPS)])
        ident = k["ident"]
        with nc.Block() as block:
            @block.tensor
            def _(pe):
                for n in range(2):
                    pe.matmul(ps[0][0:C, n, :], wv[:, :], wo[:, n * 512:(n + 1) * 512], start=True, stop=True).then_inc(folded, 1)

            @block.scalar
            def _(a):
                a.wait_ge(folded, 2)
                a.activation(vo[:, :].rearrange("p (n c) -> p n c", n=2), ps[0][0:C, 0:2, :], ACT.Copy)

            @block.vector
            def _(v):
                v.tensor_tensor(wn[:, :], wn[:, :], wn2[:, :], ALU.mult)

        phases = ["x", "turn", "xT", "q", "q_sq", "q_sum", "k", "k_sq", "k_sum", "v", "v_out", "k2", "mean", "root", "inv",
                  "k_scale", "k_turn", "k_rope", "k_fold", "kd", "q_scale", "red0", "red1", "red2", "add"]
        ch = Chain([ctx.enter_context(nc.semaphore(f"a1_step{c}")) for c in both], phases)
        hd = Chain([ctx.enter_context(nc.semaphore(f"a1_head{c}{g}")) for c, g in subs],
                   [f"{r}.{p}" for r in range(NH // NS) for p in
                    ("y", "rope", "s", "mask", "max", "nmax", "exp", "turn", "pT", "pv", "recip", "acc")])
        step, done = ch.sem, ch.after
        head, ready = dict(zip(subs, hd.sem)), hd.after
        with nc.Block() as block:
            @block.sync
            def _(sp):
                start_lanes(sp, ch)
                start_lanes(sp, hd)

            @block.tensor
            def _(pe):
                with pe.Fori(0, PAIRS) as i:
                    for c in both:
                        pe.wait_ge(step[c], done(i, "x"))
                        pe.transpose(ps[c][:, 0, 0:TP], xs[c][:, :, :].rearrange("p t c -> p (t c)"),
                                     ident[0:TP, 0:TP]).then_inc(step[c], 1)
                    for c in both:
                        pe.wait_ge(step[c], done(i, "xT"))
                        for t in range(NT):
                            for q in range(2):
                                ins = pe.matmul(ps[c][0:TP, 2 * t + q, :], xT[c][:, t * TP:(t + 1) * TP],
                                                wq[:, q * 512:(q + 1) * 512], start=True, stop=True)
                        ins.then_inc(step[c], 1)
                    for c in both:
                        pe.wait_ge(step[c], done(i, "q_sum"))
                        for t in range(NT):
                            ins = pe.matmul(ps[c][0:TP, 0, t * 2 * C:(t + 1) * 2 * C], xT[c][:, t * TP:(t + 1) * TP], wkv[:, :],
                                            start=True, stop=True)
                        ins.then_inc(step[c], 1)
                    for c in both:
                        pe.wait_ge(step[c], done(i, "k_sum"))
                        for t in range(NT):
                            for q in range(2):
                                ins = pe.matmul(ps[c][0:TP, 2 * t + q, :], xT[c][:, t * TP:(t + 1) * TP],
                                                vo[:, q * 512:(q + 1) * 512], start=True, stop=True)
                        ins.then_inc(step[c], 1)
                    for c in both:
                        pe.wait_ge(step[c], done(i, "v_out"))
                        for t in range(NT):
                            ins = pe.matmul(ps[c][0:TP, 0, t * 2 * C:(t + 1) * 2 * C], xT[c][:, t * TP:(t + 1) * TP], wkv[:, :],
                                            start=True, stop=True)
                        ins.then_inc(step[c], 1)
                    for c in both:
                        pe.wait_ge(step[c], done(i, "k_scale"))
                        for t in range(NT):
                            ins = pe.transpose(ps[c][:, 1, t * TP:(t + 1) * TP], ks[c][:, t, :], ident[0:TP, 0:TP])
                        ins.then_inc(step[c], 1)
                    for c in both:
                        pe.wait_ge(step[c], done(i, "k_rope"))
                        pe.matmul(ps[c][:, 0, 0:T], fold[:, :], kr[c][:, :], start=True, stop=True).then_inc(step[c], 1)
                    for r in range(NH // NS):
                        for c, g in subs:
                            if r == 0:
                                pe.wait_ge(step[c], done(i, "q_scale"))
                            else:
                                pe.wait_ge(head[c, g], ready(i, f"{r - 1}.acc"))
                            pe.matmul(ps[c][:, g, 0:T], wq2[:, NS * r + g, :], xT[c][:, :], start=True, stop=True).then_inc(head[c, g], 1)
                        for c, g in subs:
                            pe.wait_ge(head[c, g], ready(i, f"{r}.rope"))
                            for t in range(NT):
                                ins = pe.matmul(ps[c][0:TP, g, t * T:(t + 1) * T], y[c, g][:, t * TP:(t + 1) * TP], kd[c][:, :],
                                                start=True, stop=True)
                            ins.then_inc(head[c, g], 1)
                        for c, g in subs:
                            pe.wait_ge(head[c, g], ready(i, f"{r}.exp"))
                            for j in range(NT):
                                for t in range(NT):
                                    ins = pe.transpose(ps[c][0:TP, g, j * T + t * TP:j * T + (t + 1) * TP],
                                                       s[c, g][:, t, j * TP:(j + 1) * TP], ident[0:TP, 0:TP])
                            ins.then_inc(head[c, g], 1)
                        for c, g in subs:
                            n = NS * r + g
                            pe.wait_ge(head[c, g], ready(i, f"{r}.pT"))
                            for t in range(NT):
                                for j in range(NT):
                                    ins = pe.matmul(ps[c][0:TP, g, t * C:(t + 1) * C], pT[c, g][:, j, t * TP:(t + 1) * TP],
                                                    vs[c][:, j, n * C:(n + 1) * C], start=(j == 0), stop=(j == NT - 1))
                            ins.then_inc(head[c, g], 1)

            @block.scalar
            def _(a):
                with a.Fori(0, PAIRS) as i:
                    for c in both:
                        a.wait_ge(step[c], done(i, "turn"))
                        for t in range(NT):
                            ins = a.activation(xT[c][:, t * TP:(t + 1) * TP], ps[c][t * C:(t + 1) * C, 0, 0:TP], ACT.Copy)
                        ins.then_inc(step[c], 1)
                    for c in both:
                        a.wait_ge(step[c], done(i, "q"))
                        a.activation(sq[c][:, :, :].rearrange("p t (q n) -> p (t q) n", q=2), ps[c][0:TP, :, :], ACT.Square).then_inc(step[c], 1)
                    for c in both:
                        a.wait_ge(step[c], done(i, "k"))
                        a.activation(sq[c][:, :, 0:C], ps[c][0:TP, 0, 0:NT * 2 * C].rearrange("p (t c) -> p t c", t=NT)[:, :, 0:C],
                                     ACT.Square).then_inc(step[c], 1)
                    for c in both:
                        a.wait_ge(step[c], done(i, "v"))
                        a.activation(vs[c][:, :, :].rearrange("p t (q n) -> p (t q) n", q=2), ps[c][0:TP, :, :], ACT.Copy).then_inc(step[c], 1)
                    for c in both:
                        a.wait_ge(step[c], done(i, "mean"))
                        a.activation(rms[c][:, :, :], rms[c][:, :, :], ACT.Sqrt).then_inc(step[c], 1)
                    for c in both:
                        a.wait_ge(step[c], done(i, "k_fold"))
                        a.activation(kd[c][:, :], ps[c][:, 0, 0:T], ACT.Copy, scale=wn[:, :]).then_inc(step[c], 1)
                    for r in range(NH // NS):
                        for c, g in subs:
                            n = NS * r + g
                            a.wait_ge(head[c, g], ready(i, f"{r}.nmax"))
                            for t in range(NT):
                                ins = a.activation(s[c, g][:, t, :], s[c, g][:, t, :], ACT.Exp, bias=nmax[c, g][:, t:t + 1],
                                                   scale=rms[c][:, t, n:n + 1], accum_out=den[c, g][:, t:t + 1])
                            ins.then_inc(head[c, g], 1)
                        for c, g in subs:
                            a.wait_ge(head[c, g], ready(i, f"{r}.turn"))
                            a.activation(pT[c, g][:, :, :].rearrange("p j w -> p (j w)"), ps[c][0:TP, g, 0:NT * T],
                                         ACT.Copy).then_inc(head[c, g], 1)

            @block.vector
            def _(v):
                with v.Fori(0, PAIRS) as i:
                    tiles = [bass.ds(i * (LANES * NT) + c * NT, NT) for c in both]
                    for c in both:
                        v.wait_ge(step[c], ch.before(i))
                        v.tensor_copy(xs[c][:, :, :], xn[:, tiles[c], :]).then_inc(step[c], 1)
                    for c in both:
                        v.wait_ge(step[c], done(i, "q_sq"))
                        v.tensor_reduce(rms[c][:, :, 0:NH], sq[c][:, :, :].rearrange("p t (n c) -> p t n c", n=NH), AX.X,
                                        ALU.add).then_inc(step[c], 1)
                    for c in both:
                        v.wait_ge(step[c], done(i, "k_sq"))
                        v.tensor_reduce(rms[c][:, :, NH:NH + 1], sq[c][:, :, 0:C], AX.X, ALU.add).then_inc(step[c], 1)
                    for c in both:
                        v.wait_ge(step[c], done(i, "k2"))
                        v.tensor_scalar(rms[c][:, :, :], rms[c][:, :, :], 1.0 / C, EPS, ALU.mult, ALU.add).then_inc(step[c], 1)
                    for c in both:
                        v.wait_ge(step[c], done(i, "root"))
                        v.reciprocal(rms[c][:, :, :], rms[c][:, :, :]).then_inc(step[c], 1)
                    for c in both:
                        v.wait_ge(step[c], done(i, "inv"))
                        for t in range(NT):
                            ins = v.tensor_scalar(ks[c][:, t, :], ps[c][0:TP, 0, t * 2 * C:(t + 1) * 2 * C], rms[c][:, t, NH:NH + 1],
                                                  None, ALU.mult)
                        ins.then_inc(step[c], 1)
                    for c in both:
                        v.wait_ge(step[c], done(i, "k_turn"))
                        v.tensor_tensor(kr[c][:, :], ps[c][:, 1, 0:T], rope[:, :], ALU.mult).then_inc(step[c], 1)
                    for c in both:
                        v.wait_ge(step[c], done(i, "kd"))
                        v.tensor_scalar(rms[c][:, :, 0:NH], rms[c][:, :, 0:NH], C ** -0.5, None, ALU.mult).then_inc(step[c], 1)
                    for r in range(NH // NS):
                        for c, g in subs:
                            v.wait_ge(head[c, g], ready(i, f"{r}.y"))
                            v.tensor_tensor(y[c, g][:, :], ps[c][:, g, 0:T], rope[:, :], ALU.mult).then_inc(head[c, g], 1)
                        for c, g in subs:
                            v.wait_ge(head[c, g], ready(i, f"{r}.s"))
                            v.tensor_tensor(s[c, g][:, :, :].rearrange("p t w -> p (t w)"), ps[c][0:TP, g, 0:NT * T],
                                            mask[:, :, :].rearrange("p t w -> p (t w)"), ALU.add).then_inc(head[c, g], 1)
                            v.wait_ge(head[c, g], ready(i, f"{r}.mask"))
                            v.tensor_reduce(nmax[c, g][:, :], s[c, g][:, :, :], AX.X, ALU.max, negate=True).then_inc(head[c, g], 1)
                            v.wait_ge(head[c, g], ready(i, f"{r}.max"))
                            v.tensor_tensor(nmax[c, g][:, :], nmax[c, g][:, :], rms[c][:, :, NS * r + g], ALU.mult).then_inc(head[c, g], 1)
                        for c, g in subs:
                            v.wait_ge(head[c, g], ready(i, f"{r}.pv"))
                            v.reciprocal(den[c, g][:, :], den[c, g][:, :]).then_inc(head[c, g], 1)
                        for c, g in subs:
                            v.wait_ge(head[c, g], ready(i, f"{r}.recip"))
                            for t in range(NT):
                                out = ps[c][0:TP, g, t * C:(t + 1) * C]
                                if r == 0:
                                    ins = v.tensor_scalar(acc[c, g][:, t, :], out, den[c, g][:, t:t + 1], None, ALU.mult)
                                else:
                                    ins = v.scalar_tensor_tensor(out=acc[c, g][:, t, :], in0=out, scalar=den[c, g][:, t:t + 1],
                                                                 in1=acc[c, g][:, t, :], op0=ALU.mult, op1=ALU.add)
                            ins.then_inc(head[c, g], 1)
                    for c in both:
                        v.wait_ge(step[c], done(i, "q_scale"))
                        for g in range(NS):
                            v.wait_ge(head[c, g], ready(i, f"{NH // NS - 1}.acc"))
                        v.tensor_tensor(red[c][:, :, :], acc[c, 0][:, :, :], acc[c, 1][:, :, :], ALU.add).then_inc(step[c], 1)
                    for q in range(2):
                        for c in both:
                            v.wait_ge(step[c], done(i, f"red{q}"))
                            v.tensor_tensor(red[c][:, :, :], red[c][:, :, :], acc[c, 2 + q][:, :, :], ALU.add).then_inc(step[c], 1)
                    for c in both:
                        v.wait_ge(step[c], done(i, "red2"))
                        v.tensor_tensor(h[:, tiles[c], :], h[:, tiles[c], :], red[c][:, :, :], ALU.add).then_inc(step[c], 1)


def stage_l1_ffn(nc, h, xn, k, A):
    CA, H, NE = C + 1, 256, 8
    NC = H // 128
    with ExitStack() as ctx:
        sb = lambda n, s, d=F32: ctx.enter_context(nc.sbuf_tensor("f1_" + n, s, d))
        w1, wg, bg = sb("w1", [CA, H]), sb("wg", [128, NC, NE]), sb("bg", [TP, NE])
        wd, bd = sb("wd", [128, NC, NE, C]), sb("bd", [TP, NE, C])
        iota = sb("iota", [TP, NE])
        tick = sb("tick", [1, 2 * LANES])
        xs = [sb(f"xs{c}", [TP, NT, C]) for c in range(LANES)]
        xT = [sb(f"xT{c}", [CA, T]) for c in range(LANES)]
        hid = [sb(f"hid{c}", [128, NC, T]) for c in range(LANES)]
        lg = [sb(f"lg{c}", [TP, NT, NE]) for c in range(LANES)]
        top = [sb(f"top{c}", [TP, NT, NE]) for c in range(LANES)]
        idx = [sb(f"idx{c}", [TP, NT, NE], U32) for c in range(LANES)]
        first = [sb(f"first{c}", [TP, NT]) for c in range(LANES)]
        ex = [sb(f"ex{c}", [TP, NT, NE]) for c in range(LANES)]
        den = [sb(f"den{c}", [TP, NT]) for c in range(LANES)]
        pick = [sb(f"pick{c}", [TP, NT, NE]) for c in range(LANES)]
        y = [sb(f"y{c}", [TP, NT, NE, C]) for c in range(LANES)]
        red = [sb(f"red{c}", [TP, NT, C]) for c in range(LANES)]
        ps = [ctx.enter_context(nc.psum_tensor(f"f1_ps{c}", [128, 4, BANK], F32)) for c in range(LANES)]
        load_all(nc, ctx, "f1", [
            (w1[0:C, :], A["L1_ffn_W1"]), (w1[C:CA, :], row(A["L1_ffn_b1"])),
            (wg[:, :, :], A["L1_ffn_Wg"].rearrange("(n p) e -> p n e", p=128)),
            (bg[:, :], row(A["L1_ffn_bg"]).to_broadcast([TP, NE])),
            (bd[:, :, :].rearrange("p e c -> p (e c)"), row(A["L1_ffn_bd"].rearrange("e c -> (e c)")).to_broadcast([TP, NE * C])),
            (iota[:, :], k["iota"][0:TP, 0:NE])] + [
            (wd[:, n, :, :], A["L1_ffn_Wd"].rearrange("e (n p) c -> n p e c", p=128)[n]) for n in range(NC)],
            [(xT[c][C:CA, :], 1.0) for c in range(LANES)])
        ch = Chain([ctx.enter_context(nc.semaphore(f"f1_step{c}")) for c in range(LANES)], [
            "x", "turn", "xT", "hid", "gelu", "gate", "logits", "top", "index", "sub", "exp", "den", "recip", "pick",
            "prob", "down", "bias", "weigh", "sum", "add"])
        step, done, both = ch.sem, ch.after, range(LANES)
        with nc.Block() as block:
            @block.sync
            def _(sp):
                start_lanes(sp, ch)

            @block.tensor
            def _(pe):
                with pe.Fori(0, PAIRS) as i:
                    for c in both:
                        pe.wait_ge(step[c], done(i, "x"))
                        pe.transpose(ps[c][:, 0, 0:TP], xs[c][:, :, :].rearrange("p t c -> p (t c)"),
                                     k["ident"][0:TP, 0:TP]).then_inc(step[c], 1)
                    for c in both:
                        pe.wait_ge(step[c], done(i, "xT"))
                        for n in range(NC):
                            ins = pe.matmul(ps[c][:, 1, n * T:(n + 1) * T], w1[:, n * 128:(n + 1) * 128], xT[c][:, :],
                                            start=True, stop=True)
                        ins.then_inc(step[c], 1)
                    for c in both:
                        pe.wait_ge(step[c], done(i, "gelu"))
                        for t in range(NT):
                            for n in range(NC):
                                ins = pe.matmul(ps[c][0:TP, 0, t * NE:(t + 1) * NE], hid[c][:, n, t * TP:(t + 1) * TP],
                                                wg[:, n, :], start=(n == 0), stop=(n == NC - 1))
                        ins.then_inc(step[c], 1)
                    for c in both:
                        pe.wait_ge(step[c], done(i, "prob"))
                        for t in range(NT):
                            for n in range(NC):
                                ins = pe.matmul(ps[c][0:TP, 2 + t, :], hid[c][:, n, t * TP:(t + 1) * TP],
                                                wd[:, n, :, :].rearrange("p e c -> p (e c)"), start=(n == 0), stop=(n == NC - 1))
                        ins.then_inc(step[c], 1)

            @block.scalar
            def _(a):
                with a.Fori(0, PAIRS) as i:
                    for c in both:
                        a.wait_ge(step[c], done(i, "turn"))
                        for t in range(NT):
                            ins = a.activation(xT[c][0:C, t * TP:(t + 1) * TP], ps[c][t * C:(t + 1) * C, 0, 0:TP], ACT.Copy)
                        ins.then_inc(step[c], 1)
                    for c in both:
                        a.wait_ge(step[c], done(i, "hid"))
                        a.activation(hid[c][:, :, :].rearrange("p n w -> p (n w)"), ps[c][:, 1, 0:NC * T],
                                     ACT.Gelu).then_inc(step[c], 1)
                    for c in both:
                        a.wait_ge(step[c], done(i, "sub"))
                        a.activation(ex[c][:, :, :], ex[c][:, :, :], ACT.Exp).then_inc(step[c], 1)

            @block.vector
            def _(v):
                with v.Fori(0, PAIRS) as i:
                    tiles = [bass.ds(i * (LANES * NT) + c * NT, NT) for c in both]
                    for c in both:
                        v.wait_ge(step[c], ch.before(i))
                        v.tensor_copy(xs[c][:, :, :], xn[:, tiles[c], :]).then_inc(step[c], 1)
                    for c in both:
                        v.wait_ge(step[c], done(i, "gate"))
                        v.tensor_tensor(lg[c][:, :, :], ps[c][0:TP, 0, 0:NT * NE].rearrange("p (t e) -> p t e", t=NT),
                                        repeat(bg[:, :], NT), ALU.add).then_inc(step[c], 1)
                    for c in both:
                        v.wait_ge(step[c], done(i, "logits"))
                        v.memset(tick[:, 2 * c:2 * c + 1], 0.0)
                        for t in range(NT):
                            ins = v.max(top[c][:, t, :], lg[c][:, t, :])
                        ins.then_inc(step[c], 1)
                    for c in both:
                        v.wait_ge(step[c], done(i, "top"))
                        v.memset(tick[:, 2 * c + 1:2 * c + 2], 0.0)
                        for t in range(NT):
                            ins = v.max_index(idx[c][:, t, :], top[c][:, t, :], lg[c][:, t, :])
                        ins.then_inc(step[c], 1)
                    for c in both:
                        v.wait_ge(step[c], done(i, "index"))
                        v.tensor_copy(first[c][:, :], idx[c][:, :, 0])
                        v.tensor_tensor(ex[c][:, :, :], lg[c][:, :, :], spread(top[c][:, :, 0], NE), ALU.subtract).then_inc(step[c], 1)
                    for c in both:
                        v.wait_ge(step[c], done(i, "exp"))
                        v.tensor_reduce(den[c][:, :], ex[c][:, :, :], AX.X, ALU.add).then_inc(step[c], 1)
                    for c in both:
                        v.wait_ge(step[c], done(i, "den"))
                        v.reciprocal(den[c][:, :], den[c][:, :]).then_inc(step[c], 1)
                    for c in both:
                        v.wait_ge(step[c], done(i, "recip"))
                        v.tensor_tensor(pick[c][:, :, :], repeat(iota[:, :], NT), spread(first[c][:, :], NE), ALU.is_equal).then_inc(step[c], 1)
                    for c in both:
                        v.wait_ge(step[c], done(i, "pick"))
                        v.tensor_tensor(pick[c][:, :, :], pick[c][:, :, :], spread(den[c][:, :], NE), ALU.mult).then_inc(step[c], 1)
                    for c in both:
                        v.wait_ge(step[c], done(i, "down"))
                        for t in range(NT):
                            ins = v.tensor_tensor(y[c][:, t, :, :].rearrange("p e c -> p (e c)"), ps[c][0:TP, 2 + t, :],
                                                  bd[:, :, :].rearrange("p e c -> p (e c)"), ALU.add)
                        ins.then_inc(step[c], 1)
                    for c in both:
                        v.wait_ge(step[c], done(i, "bias"))
                        for t in range(NT):
                            ins = v.tensor_tensor(y[c][:, t, :, :], y[c][:, t, :, :], spread(pick[c][:, t, :], C), ALU.mult)
                        ins.then_inc(step[c], 1)
                    for c in both:
                        v.wait_ge(step[c], done(i, "weigh"))
                        v.tensor_reduce(red[c][:, :, :], y[c][:, :, :, :].rearrange("p t e c -> p t c e"), AX.X, ALU.add).then_inc(step[c], 1)
                    for c in both:
                        v.wait_ge(step[c], done(i, "sum"))
                        v.tensor_tensor(h[:, tiles[c], :], h[:, tiles[c], :], red[c][:, :, :], ALU.add).then_inc(step[c], 1)


def stage_l2_attn(nc, h, xn, k, A):
    NH, CA, E = 8, C + 1, 8 * C
    both = range(LANES)
    scratch = nc.dram_tensor("qkv_rows", (3 * M, E), F32, kind="Internal").ap()
    with ExitStack() as ctx:
        sb = lambda n, s, d=F32: ctx.enter_context(nc.sbuf_tensor("p2_" + n, s, d))
        w = sb("w", [CA, 3 * E])
        xs = [sb(f"xs{c}", [TP, NT, C]) for c in both]
        xT = [sb(f"xT{c}", [CA, T]) for c in both]
        q3 = [sb(f"q3{c}", [TP, NT, 3 * E]) for c in both]
        ps = [ctx.enter_context(nc.psum_tensor(f"p2_ps{c}", [128, 4, BANK], F32)) for c in both]
        load_all(nc, ctx, "p2", [(w[0:C, :], A["L2_attn_WqkvH"]), (w[C:CA, :], row(A["L2_attn_bqkvH"]))],
                 [(xT[c][C:CA, :], 1.0) for c in both])
        ch = Chain([ctx.enter_context(nc.semaphore(f"p2_step{c}")) for c in both],
                   ["x", "turn", "xT", "p0", "out0", "p1", "out1", "store:16"])
        step, done = ch.sem, ch.after
        tokens = scratch.rearrange("(b t p r) c -> p (b t) (r c)", b=B, t=NT, p=TP)
        with nc.Block() as block:
            @block.sync
            def _(sp):
                start_lanes(sp, ch)
                with sp.Fori(0, PAIRS) as i:
                    for c in both:
                        sp.wait_ge(step[c], done(i, "out1"))
                        sp.dma_start(tokens[:, bass.ds(i * (LANES * NT) + c * NT, NT), :], q3[c][:, :, :]).then_inc(step[c], 16)
                for c in both:
                    sp.wait_ge(step[c], ch.before(PAIRS))

            @block.tensor
            def _(pe):
                with pe.Fori(0, PAIRS) as i:
                    for c in both:
                        pe.wait_ge(step[c], done(i, "x"))
                        pe.transpose(ps[c][:, 3, 0:TP], xs[c][:, :, :].rearrange("p t c -> p (t c)"),
                                     k["ident"][0:TP, 0:TP]).then_inc(step[c], 1)
                    for t in range(NT):
                        for c in both:
                            pe.wait_ge(step[c], done(i, f"out{t - 1}" if t else "xT"))
                            for r in range(3):
                                ins = pe.matmul(ps[c][0:TP, r, :], xT[c][:, t * TP:(t + 1) * TP], w[:, r * E:(r + 1) * E],
                                                start=True, stop=True)
                            ins.then_inc(step[c], 1)

            @block.scalar
            def _(a):
                with a.Fori(0, PAIRS) as i:
                    for c in both:
                        a.wait_ge(step[c], done(i, "turn"))
                        for t in range(NT):
                            ins = a.activation(xT[c][0:C, t * TP:(t + 1) * TP], ps[c][t * C:(t + 1) * C, 3, 0:TP], ACT.Copy)
                        ins.then_inc(step[c], 1)
                    for c in both:
                        a.wait_ge(step[c], done(i, "p0"))
                        a.activation(q3[c][:, 0, :].rearrange("p (r n) -> p r n", r=3), ps[c][0:TP, 0:3, :], ACT.Copy).then_inc(step[c], 1)

            @block.vector
            def _(v):
                with v.Fori(0, PAIRS) as i:
                    for c in both:
                        v.wait_ge(step[c], ch.before(i))
                        v.tensor_copy(xs[c][:, :, :], xn[:, bass.ds(i * (LANES * NT) + c * NT, NT), :]).then_inc(step[c], 1)
                    for c in both:
                        v.wait_ge(step[c], done(i, "p1"))
                        v.tensor_copy(q3[c][:, 1, :].rearrange("p (r n) -> p r n", r=3), ps[c][0:TP, 0:3, :]).then_inc(step[c], 1)

    with ExitStack() as ctx:
        sb = lambda n, s, d=F32: ctx.enter_context(nc.sbuf_tensor("a2_" + n, s, d))
        w0, b0 = sb("w0", [128, 4, C]), sb("b0", [TP, C])
        qkv = [sb(f"qkv{c}", [TP, 3, NT, E]) for c in both]
        qkT = [sb(f"qkT{c}", [128, 4, 2, T]) for c in both]
        prod = [sb(f"prod{c}", [TP, NT, E]) for c in both]
        own = [sb(f"own{c}", [TP, NT, NH]) for c in both]
        nmax = [sb(f"nmax{c}", [TP, NH, NT]) for c in both]
        den = [sb(f"den{c}", [TP, NH, NT]) for c in both]
        e = [sb(f"e{c}", [TP, T]) for c in both]
        avT = [sb(f"avT{c}", [128, 4, T]) for c in both]
        red = [sb(f"red{c}", [TP, NT, C]) for c in both]
        ps = [ctx.enter_context(nc.psum_tensor(f"a2_ps{c}", [128, 4, BANK], F32)) for c in both]
        load_all(nc, ctx, "a2", [(w0[:, :, :], A["L2_attn_W0H"].rearrange("(n p) c -> p n c", p=128)),
                                 (b0[:, :], row(A["L2_attn_b0"]).to_broadcast([TP, C]))])
        phases = ["load:48", "prod", "own", "qk_turn", "qkT"]
        for g in range(2):
            phases += [f"{g}.{p}" for p in ("s", "max", "nmax")] + [f"{g}.exp{n}" for n in range(8)]
        phases += ["diff", "own_exp", "recip", "a", "av", "av_turn", "avT", "out", "bias", "add"]
        ch = Chain([ctx.enter_context(nc.semaphore(f"a2_step{c}")) for c in both], phases)
        step, done = ch.sem, ch.after
        rows = scratch.rearrange("(w b t p) c -> w p (b t) c", w=3, b=B, t=NT)
        ident = k["ident"]
        by_head = lambda ap: ap.rearrange("p n t -> p t n")
        with nc.Block() as block:
            @block.sync
            def _(sp):
                start_lanes(sp, ch)
                with sp.Fori(0, PAIRS) as i:
                    for c in both:
                        sp.wait_ge(step[c], ch.before(i))
                        for r in range(3):
                            sp.dma_start(qkv[c][:, r, :, :], rows[r, :, bass.ds(i * (LANES * NT) + c * NT, NT), :]).then_inc(step[c], 16)

            @block.tensor
            def _(pe):
                with pe.Fori(0, PAIRS) as i:
                    for c in both:
                        pe.wait_ge(step[c], done(i, "own"))
                        for p in range(4):
                            for r in range(2):
                                for t in range(NT):
                                    ins = pe.transpose(ps[c][:, p, r * T + t * TP:r * T + (t + 1) * TP],
                                                       qkv[c][:, r, t, p * 128:(p + 1) * 128], ident[0:TP, 0:TP])
                        ins.then_inc(step[c], 1)
                    for g in range(2):
                        for c in both:
                            pe.wait_ge(step[c], done(i, "0.exp7" if g else "qkT"))
                            for n in range(4):
                                p, half = (4 * g + n) // 2, slice((n % 2) * C, (n % 2 + 1) * C)
                                for t in range(NT):
                                    ins = pe.matmul(ps[c][0:TP, n, t * T:(t + 1) * T], qkT[c][half, p, 1, t * TP:(t + 1) * TP],
                                                    qkT[c][half, p, 0, :], start=True, stop=True)
                            ins.then_inc(step[c], 1)
                    for c in both:
                        pe.wait_ge(step[c], done(i, "av"))
                        for q in range(4):
                            for t in range(NT):
                                ins = pe.transpose(ps[c][:, q // 2, (q % 2) * T + t * TP:(q % 2) * T + (t + 1) * TP],
                                                   qkv[c][:, 2, t, q * 128:(q + 1) * 128], ident[0:TP, 0:TP])
                        ins.then_inc(step[c], 1)
                    for c in both:
                        pe.wait_ge(step[c], done(i, "avT"))
                        for t in range(NT):
                            for q in range(4):
                                ins = pe.matmul(ps[c][0:TP, 2, t * C:(t + 1) * C], avT[c][:, q, t * TP:(t + 1) * TP], w0[:, q, :],
                                                start=(q == 0), stop=(q == 3))
                        ins.then_inc(step[c], 1)

            @block.scalar
            def _(a):
                with a.Fori(0, PAIRS) as i:
                    for c in both:
                        a.wait_ge(step[c], done(i, "qk_turn"))
                        a.activation(qkT[c][:, :, :, :].rearrange("p q r w -> p q (r w)"), ps[c][:, :, 0:2 * T], ACT.Copy).then_inc(step[c], 1)
                    for g in range(2):
                        for n in range(8):
                            for c in both:
                                hd, t = 4 * g + n // 2, n % 2
                                a.wait_ge(step[c], done(i, f"{g}.exp{n - 1}" if n else f"{g}.nmax"))
                                a.activation(e[c][:, :], ps[c][0:TP, n // 2, t * T:(t + 1) * T], ACT.Exp, bias=nmax[c][:, hd, t:t + 1],
                                             scale=C ** -0.5, accum_out=den[c][:, hd, t:t + 1]).then_inc(step[c], 1)
                    for c in both:
                        a.wait_ge(step[c], done(i, "diff"))
                        a.activation(own[c][:, :, :], own[c][:, :, :], ACT.Exp).then_inc(step[c], 1)
                    for c in both:
                        a.wait_ge(step[c], done(i, "av_turn"))
                        a.activation(avT[c][:, :, :].rearrange("p (k q) w -> p k (q w)", k=2), ps[c][:, 0:2, 0:2 * T], ACT.Copy).then_inc(step[c], 1)

            @block.vector
            def _(v):
                with v.Fori(0, PAIRS) as i:
                    tiles = [bass.ds(i * (LANES * NT) + c * NT, NT) for c in both]
                    for c in both:
                        v.wait_ge(step[c], done(i, "load"))
                        v.tensor_tensor(prod[c][:, :, :], qkv[c][:, 0, :, :], qkv[c][:, 1, :, :], ALU.mult).then_inc(step[c], 1)
                    for c in both:
                        v.wait_ge(step[c], done(i, "prod"))
                        v.tensor_reduce(own[c][:, :, :], prod[c][:, :, :].rearrange("p t (n d) -> p t n d", n=NH), AX.X, ALU.add).then_inc(step[c], 1)
                    for g in range(2):
                        hs = slice(4 * g, 4 * g + 4)
                        for c in both:
                            v.wait_ge(step[c], done(i, f"{g}.s"))
                            v.tensor_reduce(nmax[c][:, hs, :], ps[c][0:TP, :, 0:NT * T].rearrange("p n (t w) -> p n t w", t=NT),
                                            AX.X, ALU.max).then_inc(step[c], 1)
                        for c in both:
                            v.wait_ge(step[c], done(i, f"{g}.max"))
                            v.tensor_scalar(nmax[c][:, hs, :], nmax[c][:, hs, :], -C ** -0.5, None, ALU.mult).then_inc(step[c], 1)
                    for c in both:
                        v.wait_ge(step[c], done(i, "1.exp7"))
                        v.scalar_tensor_tensor(out=own[c][:, :, :], in0=own[c][:, :, :], scalar=C ** -0.5, in1=by_head(nmax[c][:, :, :]),
                                               op0=ALU.mult, op1=ALU.add).then_inc(step[c], 1)
                    for c in both:
                        v.wait_ge(step[c], done(i, "own_exp"))
                        v.reciprocal(den[c][:, :, :], den[c][:, :, :]).then_inc(step[c], 1)
                    for c in both:
                        v.wait_ge(step[c], done(i, "recip"))
                        v.tensor_tensor(own[c][:, :, :], own[c][:, :, :], by_head(den[c][:, :, :]), ALU.mult).then_inc(step[c], 1)
                    for c in both:
                        v.wait_ge(step[c], done(i, "a"))
                        for t in range(NT):
                            val = qkv[c][:, 2, t, :].rearrange("p (n d) -> p n d", n=NH)
                            ins = v.tensor_tensor(val, val, spread(own[c][:, t, :], C), ALU.mult)
                        ins.then_inc(step[c], 1)
                    for c in both:
                        v.wait_ge(step[c], done(i, "out"))
                        v.tensor_tensor(red[c][:, :, :], ps[c][0:TP, 2, 0:NT * C].rearrange("p (t c) -> p t c", t=NT),
                                        repeat(b0[:, :], NT), ALU.add).then_inc(step[c], 1)
                    for c in both:
                        v.wait_ge(step[c], done(i, "bias"))
                        v.tensor_tensor(h[:, tiles[c], :], h[:, tiles[c], :], red[c][:, :, :], ALU.add).then_inc(step[c], 1)


def stage_l2_ffn(nc, h, xn, k, A):
    NH, E, NK, NP = 8, 8 * C, 64, 2
    TOP, SORT = 16, 24
    R = NT * NH
    KT = NK * NK // 128
    CHUNK = 2 * T
    NCH = M // CHUNK
    both = range(LANES)
    x_rows = nc.dram_tensor("pk_x_rows", (C, M), F32, kind="Internal").ap()
    t_rows = nc.dram_tensor("pk_threshold_rows", (2, NH, M), F32, kind="Internal").ap()
    with ExitStack() as outer:
        sw = outer.enter_context(nc.sbuf_tensor("pk_sw", [C, NH, 2 * NK], F32))
        with ExitStack() as ctx:
            sb = lambda n, s, d=F32: ctx.enter_context(nc.sbuf_tensor("pk_" + n, s, d))
            wpk, bd = sb("wpk", [C, NH, C]), sb("bd", [C, NH, 2 * NK])
            ps = [ctx.enter_context(nc.psum_tensor(f"pk_ps{c}", [128, 4, BANK], F32)) for c in both]
            folded = ctx.enter_context(nc.semaphore("pk_folded"))
            load_all(nc, ctx, "pk", [(wpk[:, :, :], A["L2_ffn_WpkT"])] + [
                (bd[p * 32:(p + 1) * 32, :, p * NK:(p + 1) * NK], A["L2_ffn_pkT"][p]) for p in range(NP)],
                [(bd[:, :, :], 0.0)])
            with nc.Block() as block:
                @block.tensor
                def _(pe):
                    for n in range(NH):
                        ins = pe.matmul(ps[0][0:C, n // 4, (n % 4) * 128:(n % 4 + 1) * 128], wpk[:, n, :], bd[:, n, :],
                                        start=True, stop=True)
                    ins.then_inc(folded, 1)

                @block.scalar
                def _(a):
                    a.wait_ge(folded, 1)
                    a.activation(sw[:, :, :].rearrange("p (b n) k -> p b (n k)", b=2), ps[0][0:C, 0:2, :], ACT.Copy)

            xs = [sb(f"xs{c}", [TP, NT, C]) for c in both]
            xT = [sb(f"xT{c}", [C, T]) for c in both]
            sim = [sb(f"sim{c}", [TP, R * NP, NK]) for c in both]
            srt = [sb(f"srt{c}", [TP, R, NP, SORT]) for c in both]
            RECT = ((0, 1, 24), (1, 2, 8), (3, 5, 4), (8, 16, 1))
            NCAND = sum(r * w for _, r, w in RECT)
            cand = [sb(f"cand{c}", [TP, R, NCAND]) for c in both]
            best = [sb(f"best{c}", [TP, R, SORT]) for c in both]
            eg = [sb(f"eg{c}", [TP, R, TOP + 1]) for c in both]
            low = [sb(f"low{c}", [TP, R]) for c in both]
            th = [sb(f"th{c}", [TP, R]) for c in both]
            z = [sb(f"z{c}", [TP, R]) for c in both]
            tg = [sb(f"tg{c}", [TP, 2 * R]) for c in both]
            tgT = [sb(f"tgT{c}", [2 * R, TP]) for c in both]
            tick = sb("tick", [1, LANES * 16])
            ident = k["ident"]
            phases = ["x", "turn", "xT", "xT_store:16", "sim", "sim_out", "m0", "r0", "m1", "r1", "m2", "cand",
                      "b0", "c0", "b1", "c1", "b2", "mid", "clamp", "diff", "exp", "z", "zinv", "pack", "t_turn", "t_out", "t_store:64"]
            ch = Chain([ctx.enter_context(nc.semaphore(f"pk_step{c}")) for c in both], phases)
            step, done = ch.sem, ch.after
            with nc.Block() as block:
                @block.sync
                def _(sp):
                    start_lanes(sp, ch)
                    with sp.Fori(0, PAIRS) as i:
                        for c in both:
                            sp.wait_ge(step[c], done(i, "xT"))
                            sp.dma_start(x_rows[:, bass.ds(i * (LANES * T) + c * T, T)], xT[c][:, :]).then_inc(step[c], 16)
                        for c in both:
                            sp.wait_ge(step[c], done(i, "t_out"))
                            for w in range(2):
                                for t in range(NT):
                                    q = w * R + t * NH
                                    sp.dma_start(t_rows[w, :, bass.ds(i * (LANES * T) + c * T + t * TP, TP)],
                                                 tgT[c][q:q + NH, :]).then_inc(step[c], 16)
                    for c in both:
                        sp.wait_ge(step[c], ch.before(PAIRS))

                @block.tensor
                def _(pe):
                    with pe.Fori(0, PAIRS) as i:
                        for c in both:
                            pe.wait_ge(step[c], done(i, "x"))
                            pe.transpose(ps[c][:, 0, 0:TP], xs[c][:, :, :].rearrange("p t c -> p (t c)"),
                                         ident[0:TP, 0:TP]).then_inc(step[c], 1)
                        for c in both:
                            pe.wait_ge(step[c], done(i, "xT_store"))
                            for t in range(NT):
                                for q in range(2):
                                    ins = pe.matmul(ps[c][0:TP, 2 * t + q, :], xT[c][:, t * TP:(t + 1) * TP],
                                                    sw[:, 4 * q:4 * q + 4, :].rearrange("p n k -> p (n k)"), start=True, stop=True)
                            ins.then_inc(step[c], 1)
                        for c in both:
                            pe.wait_ge(step[c], done(i, "pack"))
                            pe.matmul(ps[c][0:2 * R, 0, 0:TP], tg[c][:, :], ident[0:TP, 0:TP], start=True, stop=True).then_inc(step[c], 1)

                @block.scalar
                def _(a):
                    with a.Fori(0, PAIRS) as i:
                        for c in both:
                            a.wait_ge(step[c], done(i, "turn"))
                            for t in range(NT):
                                ins = a.activation(xT[c][:, t * TP:(t + 1) * TP], ps[c][t * C:(t + 1) * C, 0, 0:TP], ACT.Copy)
                            ins.then_inc(step[c], 1)
                        for c in both:
                            a.wait_ge(step[c], done(i, "sim"))
                            a.activation(sim[c][:, :, :].rearrange("p (q r) k -> p q (r k)", q=4), ps[c][0:TP, :, :], ACT.Copy).then_inc(step[c], 1)
                        for c in both:
                            a.wait_ge(step[c], done(i, "diff"))
                            a.activation(eg[c][:, :, :], eg[c][:, :, :], ACT.Exp).then_inc(step[c], 1)
                        for c in both:
                            a.wait_ge(step[c], done(i, "t_turn"))
                            a.activation(tgT[c][:, :], ps[c][0:2 * R, 0, 0:TP], ACT.Copy).then_inc(step[c], 1)

                @block.vector
                def _(v):
                    def hold(c, n):
                        v.memset(tick[:, c * 16 + n:c * 16 + n + 1], 0.0)

                    with v.Fori(0, PAIRS) as i:
                        for c in both:
                            v.wait_ge(step[c], ch.before(i))
                            v.tensor_copy(xs[c][:, :, :], xn[:, bass.ds(i * (LANES * NT) + c * NT, NT), :]).then_inc(step[c], 1)
                        for n in range(3):
                            for c in both:
                                v.wait_ge(step[c], done(i, f"r{n - 1}" if n else "sim_out"))
                                hold(c, 2 * n)
                                for r in range(R * NP):
                                    ins = v.max(srt[c][:, r // 2, r % 2, 8 * n:8 * n + 8], sim[c][:, r, :])
                                ins.then_inc(step[c], 1)
                            if n == 2:
                                break
                            for c in both:
                                v.wait_ge(step[c], done(i, f"m{n}"))
                                hold(c, 2 * n + 1)
                                for r in range(R * NP):
                                    ins = v.match_replace(sim[c][:, r, :], srt[c][:, r // 2, r % 2, 8 * n:8 * n + 8], sim[c][:, r, :], NEG)
                                ins.then_inc(step[c], 1)
                        for c in both:
                            v.wait_ge(step[c], done(i, "m2"))
                            at = 0
                            for a0, rows, w in RECT:
                                dst = cand[c][:, :, at:at + rows * w].rearrange("p r (a b) -> p r a b", b=w)
                                ins = v.tensor_tensor(dst, spread(srt[c][:, :, 0, a0:a0 + rows], w),
                                                      srt[c][:, :, 1, 0:w].unsqueeze(2).to_broadcast([TP, R, rows, w]), ALU.add)
                                at += rows * w
                            ins.then_inc(step[c], 1)
                        for n in range(3):
                            for c in both:
                                v.wait_ge(step[c], done(i, f"c{n - 1}" if n else "cand"))
                                hold(c, 8 + 2 * n)
                                for r in range(R):
                                    ins = v.max(best[c][:, r, 8 * n:8 * n + 8], cand[c][:, r, :])
                                ins.then_inc(step[c], 1)
                            if n == 2:
                                break
                            for c in both:
                                v.wait_ge(step[c], done(i, f"b{n}"))
                                hold(c, 9 + 2 * n)
                                for r in range(R):
                                    ins = v.match_replace(cand[c][:, r, :], best[c][:, r, 8 * n:8 * n + 8], cand[c][:, r, :], NEG)
                                ins.then_inc(step[c], 1)
                        for c in both:
                            v.wait_ge(step[c], done(i, "b2"))
                            v.tensor_tensor(th[c][:, :], best[c][:, :, TOP - 1], best[c][:, :, TOP], ALU.add)
                            v.tensor_scalar(low[c][:, :], best[c][:, :, 0], -80.0, None, ALU.add).then_inc(step[c], 1)
                        for c in both:
                            v.wait_ge(step[c], done(i, "mid"))
                            v.scalar_tensor_tensor(out=th[c][:, :], in0=th[c][:, :], scalar=0.5, in1=low[c][:, :],
                                                   op0=ALU.mult, op1=ALU.max).then_inc(step[c], 1)
                        for c in both:
                            v.wait_ge(step[c], done(i, "clamp"))
                            v.tensor_tensor(eg[c][:, :, 0:TOP], best[c][:, :, 0:TOP], spread(best[c][:, :, 0], TOP), ALU.subtract)
                            v.tensor_scalar(tg[c][:, 0:R], th[c][:, :], -1.0, None, ALU.mult)
                            v.tensor_tensor(eg[c][:, :, TOP], th[c][:, :], best[c][:, :, 0], ALU.subtract).then_inc(step[c], 1)
                        for c in both:
                            v.wait_ge(step[c], done(i, "exp"))
                            v.tensor_reduce(z[c][:, :], eg[c][:, :, 0:TOP], AX.X, ALU.add).then_inc(step[c], 1)
                        for c in both:
                            v.wait_ge(step[c], done(i, "z"))
                            v.reciprocal(z[c][:, :], z[c][:, :]).then_inc(step[c], 1)
                        for c in both:
                            v.wait_ge(step[c], done(i, "zinv"))
                            v.tensor_tensor(tg[c][:, R:2 * R], z[c][:, :], eg[c][:, :, TOP], ALU.mult).then_inc(step[c], 1)

        with ExitStack() as ctx:
            sb = lambda n, s, d=F32: ctx.enter_context(nc.sbuf_tensor("pm_" + n, s, d))
            sem = lambda n: ctx.enter_context(nc.semaphore("pm_" + n))
            PARTS = 3
            ROWS = PARTS * 32
            NG = 8
            NB = 3
            tab, keys = sb("tab", [128, KT, 2 * C]), sb("keys", [C + 1, 4, PARTS, 32])
            picks, pick = sb("picks", [ROWS, NG + 1, 128]), sb("pick", [ROWS, NG + 1, 128], BF16)
            xb = sb("xb", [C + 1, CHUNK])
            score = sb("score", [ROWS, NCH, 4, CHUNK], BF16)
            rest = [sb(f"rest{c}", [ROWS, 2, CHUNK]) for c in both]
            mid = [sb(f"mid{c}", [ROWS, 2, CHUNK], BF16) for c in both]
            wq, wo = sb("wq", [C, C]), sb("wo", [128, C])
            xa, gb = sb("xa", [C, CHUNK]), sb("gb", [128, CHUNK])
            e, w = sb("e", [128, NB, CHUNK]), sb("w", [128, NB, CHUNK])
            mask = sb("mask", [TP, NT, T])
            kv = [sb(f"kv{c}", [128, T]) for c in both]
            q = [sb(f"q{c}", [C, T]) for c in both]
            vp = [sb(f"vp{c}", [TP, NT, C]) for c in both]
            s = [sb(f"s{c}", [TP, NT, T]) for c in both]
            pT = [sb(f"pT{c}", [TP, NT, T]) for c in both]
            nmax = [sb(f"nmax{c}", [TP, NT]) for c in both]
            den = [sb(f"den{c}", [TP, NT]) for c in both]
            red = [sb(f"red{c}", [TP, NT, C]) for c in both]
            sums = ctx.enter_context(nc.psum_tensor("pm_sums", [128, NB, BANK], F32))
            out = ctx.enter_context(nc.psum_tensor("pm_out", [128, BANK], F32))
            ps = [ctx.enter_context(nc.psum_tensor(f"pm_ps{c}", [128, 2, BANK], F32)) for c in both]
            load_all(nc, ctx, "pm", [(mask[:, :, :], k["causal"]), (picks[:, :, :], k["picks"])],
                     [(keys[C:C + 1, 2 * c:2 * c + 2, :, :], float(c)) for c in both])
            sums_ready, exp_ready = sem("sums_ready"), sem("exp_ready")
            weights_ready, used = sem("weights_ready"), sem("weights_used")
            head_ready = Chain([sem("head_step")], ["load:48", "keys"])
            hs = head_ready.sem[0]
            chunk_loaded = sem("chunk_loaded")
            xb_loaded, picks_ready = sem("xb_loaded"), sem("picks_ready")
            pre = Chain([sem(f"score_step{c}") for c in both], ["rows", "part0", "rest", "part1", "part2"])
            scored = lambda it, name: pre.after(it, name) + pre.per
            SCORE_SLOT = {"rows": 23, "part0": 25, "rest": 26, "part1": 28, "part2": 30}
            ch = Chain([sem(f"step{c}") for c in both], [
                "kv", "qv", "qv_out", "s", "mask", "max", "nmax", "exp", "turn", "pT", "pv", "recip", "norm", "add"])
            step, START = ch.sem, ch.per
            done = lambda it, name: ch.after(it, name) + START
            SLOT = {n: 1 + 2 * p for p, n in enumerate(("s", "mask", "max", "nmax", "exp", "turn", "pT", "pv", "recip", "norm", "add"))}

            def chunks(eng, head, body, last):
                with eng.Fori(0, NH) as hd:
                    head(hd)
                    body(hd * NCH, hd, 0, False, True)
                    with eng.Fori(1, NCH - 1) as ck:
                        body(hd * NCH + ck, hd, ck, True, True)
                    body(hd * NCH + (NCH - 1), hd, NCH - 1, True, False)
                    last(hd * NCH + (NCH - 1), hd)

            with nc.Block() as block:
                @block.sync
                def _(sp):
                    for c in both:
                        sp.sem_inc(step[c], START + 1)
                        sp.sem_inc(pre.sem[c], pre.per + 1)
                    sp.sem_inc(hs, 1)
                    sp.sem_inc(weights_ready, NB)
                    sp.sem_inc(used, NB)

                    def head(hd):
                        for c in both:
                            sp.wait_ge(step[c], done(hd * NCH, "add") - ch.per)
                        sp.dma_start(tab[:, :, :], A["L2_ffn_tables"][bass.ds(hd, 1)].rearrange("a p t c -> (a p) t c")).then_inc(hs, 16)
                        sp.dma_start(wq[:, :], A["L2_ffn_Wq"][:, bass.ds(hd * C, C)]).then_inc(hs, 16)
                        sp.dma_start(wo[C:2 * C, :], A["L2_ffn_WoH"][bass.ds(hd, 1)].rearrange("a p c -> (a p) c")).then_inc(hs, 16)

                    def body(it, hd, ck, previous, more):
                        def ahead(it, ck):
                            for c in both:
                                sp.wait_ge(pre.sem[c], scored(it, "rows") - pre.per)
                            sp.dma_start(xb[0:C, :], x_rows[:, bass.ds(ck * CHUNK, CHUNK)]).then_inc(xb_loaded, 16)
                            sp.dma_start(xb[C:C + 1, :], t_rows[0, bass.ds(hd, 1), bass.ds(ck * CHUNK, CHUNK)]).then_inc(xb_loaded, 16)

                        if not previous:
                            ahead(it, ck)
                        if more:
                            ahead(it + 1, ck + 1)
                        for c in both:
                            sp.wait_ge(step[c], done(it, "qv") - ch.per)
                        sp.dma_start(xa[:, :], x_rows[:, bass.ds(ck * CHUNK, CHUNK)]).then_inc(chunk_loaded, 16)
                        sp.dma_start(gb[:, :], t_rows[1, bass.ds(hd, 1), bass.ds(ck * CHUNK, CHUNK)].to_broadcast([128, CHUNK])).then_inc(chunk_loaded, 16)

                    chunks(sp, head, body, lambda it, hd: None)

                @block.tensor
                def _(pe):
                    def attend(it, name):
                        for c in both:
                            if name == "s":
                                pe.wait_ge(step[c], done(it, "qv_out"))
                                for t in range(NT):
                                    ins = pe.matmul(ps[c][0:TP, 1, t * T:(t + 1) * T], q[c][:, t * TP:(t + 1) * TP], kv[c][0:C, :],
                                                    start=True, stop=True)
                                ins.then_inc(step[c], 1)
                            elif name == "turn":
                                pe.wait_ge(step[c], done(it, "exp"))
                                for j in range(NT):
                                    for t in range(NT):
                                        ins = pe.transpose(ps[c][0:TP, 0, j * T + t * TP:j * T + (t + 1) * TP],
                                                           s[c][:, t, j * TP:(j + 1) * TP], ident[0:TP, 0:TP])
                                ins.then_inc(step[c], 1)
                            elif name == "pv":
                                pe.wait_ge(step[c], done(it, "pT"))
                                for t in range(NT):
                                    for j in range(NT):
                                        ins = pe.matmul(ps[c][0:TP, 1, t * C:(t + 1) * C], pT[c][:, j, t * TP:(t + 1) * TP],
                                                        vp[c][:, j, :], start=(j == 0), stop=(j == NT - 1))
                                ins.then_inc(step[c], 1)

                    def head(hd):
                        pe.wait_ge(picks_ready, 1)
                        pe.wait_ge(hs, head_ready.after(hd, "keys"))

                    def body(it, hd, ck, previous, more):
                        def rows(it):
                            pe.wait_ge(xb_loaded, it * 32 + 32)
                            for c in both:
                                for j in range(2):
                                    ins = pe.matmul(ps[c][0:ROWS, j, 0:CHUNK], keys[:, 2 * c + j, :, :].rearrange("p a b -> p (a b)"), xb[:, :],
                                                    start=True, stop=True)
                                ins.then_inc(pre.sem[c], 1)

                        def make(t):
                            pe.wait_ge(weights_ready, it * KT + t + 1)
                            part = lambda q: score[:, bass.ds(ck, 1), q, :].rearrange("p a w -> p (a w)")
                            pe.matmul(sums[:, t % NB, 0:CHUNK], pick[:, t // 2 % NG, :], part(2 + t // 2 // NG), start=True, stop=False)
                            pe.matmul(sums[:, t % NB, 0:CHUNK], pick[:, NG, :], part(t % 2), start=False, stop=True).then_inc(sums_ready, 1)

                        if not previous:
                            for c in both:
                                pe.wait_ge(step[c], done(it, "add") - ch.per)
                            rows(it)
                        for c in both:
                            pe.wait_ge(pre.sem[c], scored(it, "part2"))

                        for t in range(KT + 2):
                            if t < KT:
                                make(t)
                            if t >= 2:
                                g = t - 2
                                if g == 0:
                                    for c in both:
                                        pe.wait_ge(step[c], done(it, "kv") - ch.per)
                                pe.wait_ge(weights_ready, it * KT + (g + 1 + NB))
                                pe.matmul(out[:, 0:CHUNK], tab[:, g, :], w[:, g % NB, :], start=(g == 0), stop=(g == KT - 1)).then_inc(used, 1)
                            if previous:
                                for name, at in SLOT.items():
                                    if at == t:
                                        attend(it - 1, name)
                            if more and t == SCORE_SLOT["rows"]:
                                for c in both:
                                    pe.wait_ge(step[c], done(it, "add") - ch.per)
                                rows(it + 1)
                        pe.wait_ge(chunk_loaded, it * 32 + 32)
                        if more:
                            for c in both:
                                pe.wait_ge(pre.sem[c], scored(it + 1, "rest"))
                        for c in both:
                            pe.wait_ge(step[c], done(it, "kv"))
                            for t in range(NT):
                                pe.matmul(ps[c][0:TP, 1, t * C:(t + 1) * C], kv[c][C:2 * C, t * TP:(t + 1) * TP], wo[C:2 * C, :],
                                          start=True, stop=True)
                            pe.matmul(ps[c][0:C, 0, 0:T], wq[:, :], xa[0:C, c * T:(c + 1) * T], start=True, stop=True).then_inc(step[c], 1)

                    chunks(pe, head, body, lambda it, hd: [attend(it, n) for n in SLOT])

                @block.scalar
                def _(a):
                    def attend(it, name):
                        for c in both:
                            if name == "exp":
                                a.wait_ge(step[c], done(it, "nmax"))
                                for t in range(NT):
                                    ins = a.activation(s[c][:, t, :], s[c][:, t, :], ACT.Exp, bias=nmax[c][:, t:t + 1],
                                                       scale=C ** -0.5, accum_out=den[c][:, t:t + 1])
                                ins.then_inc(step[c], 1)
                            elif name == "pT":
                                a.wait_ge(step[c], done(it, "turn"))
                                a.activation(pT[c][:, :, :].rearrange("p j w -> p (j w)"), ps[c][0:TP, 0, 0:NT * T],
                                             ACT.Copy).then_inc(step[c], 1)

                    def body(it, hd, ck, previous, more):
                        def prepare(it, ck, name):
                            for c in both:
                                mine = lambda p: score[p * 32:p * 32 + 32, bass.ds(ck, 1), 2 * c:2 * c + 2, :].rearrange("p a q w -> p (a q) w")
                                if name == "part0":
                                    a.wait_ge(pre.sem[c], scored(it, "rows"))
                                    a.activation(score[:, bass.ds(ck, 1), 2 * c:2 * c + 2, :].rearrange("p a q w -> p (a q) w"),
                                                 ps[c][0:ROWS, 0:2, 0:CHUNK], ACT.Copy).then_inc(pre.sem[c], 1)
                                elif name == "part1":
                                    a.wait_ge(pre.sem[c], scored(it, "rest"))
                                    a.activation(mine(1), rest[c][32:64, :, :], ACT.Copy)
                                    a.activation(mid[c][64:96, :, :], rest[c][64:96, :, :], ACT.Copy).then_inc(pre.sem[c], 1)

                        if not previous:
                            for name in SCORE_SLOT:
                                prepare(it, ck, name)
                        for t in range(KT):
                            a.wait_ge(sums_ready, it * KT + t + 1)
                            a.wait_ge(weights_ready, it * KT + t + 1)
                            a.activation(e[:, t % NB, :], sums[:, t % NB, 0:CHUNK], ACT.Exp).then_inc(exp_ready, 1)
                            if previous:
                                for name, at in SLOT.items():
                                    if at == t:
                                        attend(it - 1, name)
                            if more:
                                for name, at in SCORE_SLOT.items():
                                    if at == t:
                                        prepare(it + 1, ck + 1, name)
                        for c in both:
                            a.wait_ge(step[c], done(it, "qv"))
                            a.activation(q[c][:, :], ps[c][0:C, 0, 0:T], ACT.Copy)
                            a.activation(vp[c][:, :, :].rearrange("p t c -> p (t c)"), ps[c][0:TP, 1, 0:NT * C], ACT.Copy).then_inc(step[c], 1)

                    chunks(a, lambda hd: None, body, lambda it, hd: [attend(it, n) for n in SLOT])

                @block.vector
                def _(v):
                    def attend(it, name, ck):
                        for c in both:
                            if name == "mask":
                                v.wait_ge(step[c], done(it, "s"))
                                v.tensor_tensor(s[c][:, :, :].rearrange("p t w -> p (t w)"), ps[c][0:TP, 1, 0:NT * T],
                                                mask[:, :, :].rearrange("p t w -> p (t w)"), ALU.add).then_inc(step[c], 1)
                            elif name == "max":
                                v.wait_ge(step[c], done(it, "mask"))
                                v.tensor_reduce(nmax[c][:, :], s[c][:, :, :], AX.X, ALU.max).then_inc(step[c], 1)
                            elif name == "nmax":
                                v.wait_ge(step[c], done(it, "max"))
                                v.tensor_scalar(nmax[c][:, :], nmax[c][:, :], -C ** -0.5, None, ALU.mult).then_inc(step[c], 1)
                            elif name == "recip":
                                v.wait_ge(step[c], done(it, "pv"))
                                v.reciprocal(den[c][:, :], den[c][:, :]).then_inc(step[c], 1)
                            elif name == "norm":
                                v.wait_ge(step[c], done(it, "recip"))
                                v.tensor_tensor(red[c][:, :, :], ps[c][0:TP, 1, 0:NT * C].rearrange("p (t c) -> p t c", t=NT),
                                                spread(den[c][:, :], C), ALU.mult).then_inc(step[c], 1)
                            elif name == "add":
                                v.wait_ge(step[c], done(it, "norm"))
                                tiles = bass.ds(ck * (LANES * NT) + c * NT, NT)
                                v.tensor_tensor(h[:, tiles, :], h[:, tiles, :], red[c][:, :, :], ALU.add).then_inc(step[c], 1)

                    v.tensor_copy(pick[:, :, :], picks[:, :, :]).then_inc(picks_ready, 1)

                    def head(hd):
                        v.wait_ge(hs, head_ready.after(hd, "load"))
                        halves = sw[:, bass.ds(hd, 1), :].rearrange("p a k -> p (a k)")
                        v.tensor_copy(keys[0:C, :, :, :], halves.rearrange("p (q k) -> p q k", q=4).unsqueeze(2).to_broadcast(
                            [C, 4, PARTS, 32])).then_inc(hs, 1)

                    def body(it, hd, ck, previous, more):
                        def prepare(it, ck, name):
                            for c in both:
                                mine = score[:, bass.ds(ck, 1), 2 * c:2 * c + 2, :].rearrange("p a q w -> p (a q) w")
                                if name == "rest":
                                    v.wait_ge(pre.sem[c], scored(it, "part0"))
                                    v.tensor_tensor(rest[c][:, :, :], ps[c][0:ROWS, 0:2, 0:CHUNK], mine, ALU.subtract).then_inc(pre.sem[c], 1)
                                elif name == "part2":
                                    v.wait_ge(pre.sem[c], scored(it, "part1"))
                                    v.tensor_tensor(mine[64:96], rest[c][64:96, :, :], mid[c][64:96, :, :], ALU.subtract).then_inc(pre.sem[c], 1)

                        if not previous:
                            for name in SCORE_SLOT:
                                prepare(it, ck, name)
                        for t in range(KT):
                            v.wait_ge(exp_ready, it * KT + t + 1)
                            v.wait_ge(used, it * KT + t + 1)
                            v.scalar_tensor_tensor(out=w[:, t % NB, :], in0=sums[:, t % NB, 0:CHUNK], scalar=0.0, in1=e[:, t % NB, :],
                                                   op0=ALU.is_gt, op1=ALU.mult).then_inc(weights_ready, 1)
                            if previous:
                                for name, at in SLOT.items():
                                    if at == t:
                                        attend(it - 1, name, ck - 1)
                            if more:
                                for name, at in SCORE_SLOT.items():
                                    if at == t:
                                        prepare(it + 1, ck + 1, name)
                        v.wait_ge(used, it * KT + (KT + NB))
                        v.wait_ge(chunk_loaded, it * 32 + 32)
                        for c in both:
                            v.wait_ge(step[c], done(it, "add") - ch.per)
                            v.tensor_tensor(kv[c][:, :], out[:, c * T:(c + 1) * T], gb[:, c * T:(c + 1) * T], ALU.mult).then_inc(step[c], 1)

                    chunks(v, head, body, lambda it, hd: [attend(it, n, NCH - 1) for n in SLOT])


def stage_l3_attn(nc, h, xn, k, A):
    NH, D, CA = 8, 32, C + 1
    INNER = NH * D
    NC = INNER // 128
    with ExitStack() as ctx:
        xn2 = ctx.enter_context(nc.sbuf_tensor("xn2", [TP, TILES, C], F32))
        layernorm_all(nc, xn, xn2, "s7b")
        sb = lambda n, s, d=F32: ctx.enter_context(nc.sbuf_tensor("a3_" + n, s, d))
        wq, wk = sb("wq", [D, NH, C]), sb("wk", [D, NH, C])
        wv, wg = sb("wv", [C, INNER]), sb("wg", [CA, INNER])
        wf, bf = sb("wf", [128, NC, C]), sb("bf", [TP, C])
        gamma, beta = sb("gamma", [C, 1]), sb("beta", [C, 1])
        m = sb("m", [C, NH, CA])
        xs = [sb(f"xs{c}", [TP, 2 * NT, C]) for c in range(LANES)]
        xT = [sb(f"xT{c}", [C, T]) for c in range(LANES)]
        hT = [sb(f"hT{c}", [CA, T]) for c in range(LANES)]
        vs = [sb(f"vs{c}", [TP, NT, INNER]) for c in range(LANES)]
        gate = [sb(f"gate{c}", [TP, NT, INNER]) for c in range(LANES)]
        NS = 4
        subs = [(c, g) for g in range(NS) for c in range(LANES)]
        per = lambda n, shape: {cg: sb(f"{n}{cg[0]}{cg[1]}", shape) for cg in subs}
        vr, y, s = per("vr", [TP, NT, D]), per("y", [C, T]), per("s", [TP, NT, T])
        nmax, den = per("nmax", [TP, NT]), per("den", [TP, NT])
        oT = [sb(f"oT{c}", [128, NC, T]) for c in range(LANES)]
        red = [sb(f"red{c}", [TP, NT, C]) for c in range(LANES)]
        ps = [ctx.enter_context(nc.psum_tensor(f"a3_ps{c}", [128, 4, BANK], F32)) for c in range(LANES)]
        folded = ctx.enter_context(nc.semaphore("a3_folded"))
        moved = ctx.enter_context(nc.semaphore("a3_fold_moved"))
        load_all(nc, ctx, "a3", [
            (wq[:, :, :], A["L3_attn_WqH"]), (wk[:, :, :], A["L3_attn_WkH"]), (wv[:, :], A["L3_attn_WvT"]),
            (wg[0:C, :], A["L3_attn_WgT"]), (wg[C:CA, :], row(A["L3_attn_b_gate"])),
            (wf[:, :, :], A["L3_attn_WfT"].rearrange("(n p) c -> p n c", p=128)),
            (bf[:, :], row(A["L3_attn_b_final"]).to_broadcast([TP, C])),
            (gamma[:, :], A["L3_attn_ln_gamma"].rearrange("(n a) -> n a", a=1)),
            (beta[:, :], A["L3_attn_ln_beta"].rearrange("(n a) -> n a", a=1))],
            [(hT[c][C:CA, :], 1.0) for c in range(LANES)] + [(m[:, :, :], 0.0)])
        ident = k["ident"]
        with nc.Block() as block:
            @block.tensor
            def _(pe):
                for n in range(NH):
                    pe.matmul(ps[0][0:C, n % 4, 0:C], wq[:, n, :], wk[:, n, :], start=True, stop=True).then_inc(folded, 1)
                    pe.wait_ge(moved, n + 1)

            @block.scalar
            def _(a):
                for n in range(NH):
                    a.wait_ge(folded, n + 1)
                    a.activation(m[:, n, 0:C], ps[0][0:C, n % 4, 0:C], ACT.Copy).then_inc(moved, 1)

        ch = Chain([ctx.enter_context(nc.semaphore(f"a3_step{c}")) for c in range(LANES)],
                   ["x", "turn", "xT", "hT", "vg", "v_out", "gate", "o_turn", "oT", "final", "bias", "res", "add"])
        hd = Chain([ctx.enter_context(nc.semaphore(f"a3_head{c}{g}")) for c, g in subs],
                   [f"{r}.{p}" for r in range(NH // NS) for p in
                    ("y", "y_out", "s", "max", "nmax", "exp", "recip", "vr", "pv", "gated")])
        step, done, both = ch.sem, ch.after, range(LANES)
        head, ready = dict(zip(subs, hd.sem)), hd.after
        with nc.Block() as block:
            @block.sync
            def _(sp):
                start_lanes(sp, ch)
                start_lanes(sp, hd)

            @block.tensor
            def _(pe):
                with pe.Fori(0, PAIRS) as i:
                    for c in both:
                        pe.wait_ge(step[c], done(i, "x"))
                        for q in range(2):
                            ins = pe.transpose(ps[c][:, 0, q * TP:(q + 1) * TP],
                                               xs[c][:, q * NT:(q + 1) * NT, :].rearrange("p t c -> p (t c)"), ident[0:TP, 0:TP])
                        ins.then_inc(step[c], 1)
                    for c in both:
                        pe.wait_ge(step[c], done(i, "hT"))
                        for t in range(NT):
                            pe.matmul(ps[c][0:TP, 1, t * INNER:(t + 1) * INNER], xT[c][:, t * TP:(t + 1) * TP], wv[:, :], start=True, stop=True)
                            ins = pe.matmul(ps[c][0:TP, 2, t * INNER:(t + 1) * INNER], hT[c][:, t * TP:(t + 1) * TP], wg[:, :], start=True, stop=True)
                        ins.then_inc(step[c], 1)
                    for r in range(NH // NS):
                        for c, g in subs:
                            if r == 0:
                                pe.wait_ge(step[c], done(i, "gate"))
                            else:
                                pe.wait_ge(head[c, g], ready(i, f"{r - 1}.gated"))
                            pe.matmul(ps[c][0:CA, g, 0:T], m[:, NS * r + g, :], xT[c][:, :], start=True, stop=True).then_inc(head[c, g], 1)
                        for c, g in subs:
                            pe.wait_ge(head[c, g], ready(i, f"{r}.y_out"))
                            for t in range(NT):
                                ins = pe.matmul(ps[c][0:TP, g, t * T:(t + 1) * T], y[c, g][:, t * TP:(t + 1) * TP], xT[c][:, :],
                                                start=True, stop=True)
                            ins.then_inc(head[c, g], 1)
                        for c, g in subs:
                            pe.wait_ge(head[c, g], ready(i, f"{r}.vr"))
                            for j in range(NT):
                                for t in range(NT):
                                    ins = pe.matmul(ps[c][0:TP, g, j * D:(j + 1) * D],
                                                    s[c, g][:, t, j * TP:(j + 1) * TP], vr[c, g][:, t, :], start=(t == 0), stop=(t == NT - 1))
                            ins.then_inc(head[c, g], 1)
                    for c in both:
                        for g in range(NS):
                            pe.wait_ge(head[c, g], ready(i, f"{NH // NS - 1}.gated"))
                        for q in range(NC):
                            for t in range(NT):
                                ins = pe.transpose(ps[c][:, 0, q * T + t * TP:q * T + (t + 1) * TP],
                                                   gate[c][:, t, q * 128:(q + 1) * 128], ident[0:TP, 0:TP])
                        ins.then_inc(step[c], 1)
                    for c in both:
                        pe.wait_ge(step[c], done(i, "oT"))
                        for t in range(NT):
                            for q in range(NC):
                                ins = pe.matmul(ps[c][0:TP, 1, t * C:(t + 1) * C], oT[c][:, q, t * TP:(t + 1) * TP], wf[:, q, :],
                                                start=(q == 0), stop=(q == NC - 1))
                        ins.then_inc(step[c], 1)

            @block.scalar
            def _(a):
                with a.Fori(0, PAIRS) as i:
                    for c in both:
                        a.wait_ge(step[c], done(i, "turn"))
                        for t in range(NT):
                            ins = a.activation(xT[c][:, t * TP:(t + 1) * TP], ps[c][t * C:(t + 1) * C, 0, 0:TP], ACT.Identity,
                                               bias=beta[:, :], scale=gamma[:, :])
                        ins.then_inc(step[c], 1)
                    for c in both:
                        a.wait_ge(step[c], done(i, "xT"))
                        for t in range(NT):
                            ins = a.activation(hT[c][0:C, t * TP:(t + 1) * TP], ps[c][t * C:(t + 1) * C, 0, TP:2 * TP], ACT.Copy)
                        ins.then_inc(step[c], 1)
                    for c in both:
                        a.wait_ge(step[c], done(i, "vg"))
                        a.activation(vs[c][:, :, :].rearrange("p t c -> p (t c)"), ps[c][0:TP, 1, 0:NT * INNER], ACT.Copy).then_inc(step[c], 1)
                    for c in both:
                        a.wait_ge(step[c], done(i, "v_out"))
                        a.activation(gate[c][:, :, :].rearrange("p t c -> p (t c)"), ps[c][0:TP, 2, 0:NT * INNER],
                                     ACT.Sigmoid).then_inc(step[c], 1)
                    for r in range(NH // NS):
                        for c, g in subs:
                            a.wait_ge(head[c, g], ready(i, f"{r}.y"))
                            a.activation(y[c, g][:, :], ps[c][0:C, g, 0:T], ACT.Copy).then_inc(head[c, g], 1)
                        for c, g in subs:
                            a.wait_ge(head[c, g], ready(i, f"{r}.nmax"))
                            for t in range(NT):
                                ins = a.activation(s[c, g][:, t, :], ps[c][0:TP, g, t * T:(t + 1) * T], ACT.Exp, bias=nmax[c, g][:, t:t + 1],
                                                   scale=D ** -0.5, accum_out=den[c, g][:, t:t + 1])
                            ins.then_inc(head[c, g], 1)
                    for c in both:
                        a.wait_ge(step[c], done(i, "o_turn"))
                        a.activation(oT[c][:, :, :].rearrange("p q w -> p (q w)"), ps[c][:, 0, 0:NC * T], ACT.Copy).then_inc(step[c], 1)

            @block.vector
            def _(v):
                with v.Fori(0, PAIRS) as i:
                    tiles = [bass.ds(i * (LANES * NT) + c * NT, NT) for c in both]
                    for c in both:
                        v.wait_ge(step[c], ch.before(i))
                        v.tensor_copy(xs[c][:, 0:NT, :], xn2[:, tiles[c], :])
                        v.tensor_copy(xs[c][:, NT:2 * NT, :], xn[:, tiles[c], :]).then_inc(step[c], 1)
                    for r in range(NH // NS):
                        for c, g in subs:
                            v.wait_ge(head[c, g], ready(i, f"{r}.s"))
                            v.tensor_reduce(nmax[c, g][:, :], ps[c][0:TP, g, 0:NT * T].rearrange("p (t w) -> p t w", t=NT),
                                            AX.X, ALU.max).then_inc(head[c, g], 1)
                            v.wait_ge(head[c, g], ready(i, f"{r}.max"))
                            v.tensor_scalar(nmax[c, g][:, :], nmax[c, g][:, :], -D ** -0.5, None, ALU.mult).then_inc(head[c, g], 1)
                        for c, g in subs:
                            n = NS * r + g
                            v.wait_ge(head[c, g], ready(i, f"{r}.exp"))
                            v.reciprocal(den[c, g][:, :], den[c, g][:, :]).then_inc(head[c, g], 1)
                            v.wait_ge(head[c, g], ready(i, f"{r}.recip"))
                            v.tensor_tensor(vr[c, g][:, :, :], vs[c][:, :, n * D:(n + 1) * D], spread(den[c, g][:, :], D), ALU.mult).then_inc(head[c, g], 1)
                        for c, g in subs:
                            n = NS * r + g
                            v.wait_ge(head[c, g], ready(i, f"{r}.pv"))
                            part = gate[c][:, :, n * D:(n + 1) * D]
                            v.tensor_tensor(part, ps[c][0:TP, g, 0:NT * D].rearrange("p (t d) -> p t d", t=NT), part,
                                            ALU.mult).then_inc(head[c, g], 1)
                    for c in both:
                        v.wait_ge(step[c], done(i, "final"))
                        v.tensor_tensor(red[c][:, :, :], ps[c][0:TP, 1, 0:NT * C].rearrange("p (t c) -> p t c", t=NT),
                                        repeat(bf[:, :], NT), ALU.add).then_inc(step[c], 1)
                    for c in both:
                        v.wait_ge(step[c], done(i, "bias"))
                        v.tensor_tensor(red[c][:, :, :], red[c][:, :, :], xs[c][:, NT:2 * NT, :], ALU.add).then_inc(step[c], 1)
                    for c in both:
                        v.wait_ge(step[c], done(i, "res"))
                        v.tensor_tensor(h[:, tiles[c], :], h[:, tiles[c], :], red[c][:, :, :], ALU.add).then_inc(step[c], 1)


def stage_l3_ffn(nc, h, xn, k, A):
    NHD, NE = 4, 4
    HE = NHD * NE
    RW = NHD * (NE + 1)
    SRC = RW + 2 * NHD
    DST = 2 * NHD
    ED = A["L3_ffn_edge_index"].shape[1]
    CH = ED // 128
    LO = 128
    HI = -(-M // LO)
    RANGE = 40.0
    SETS = 128 // RW
    PARTS = 3
    rows = nc.dram_tensor("gat_sources", (M, SRC), F32, kind="Internal").ap()
    drows = nc.dram_tensor("gat_targets", (M, DST), F32, kind="Internal").ap()
    kept = nc.dram_tensor("gat_edge_rows", (128, CH, SRC), F32, kind="Internal").ap()
    csum = nc.dram_tensor("gat_c_sums", (HI * LO, NHD), F32, kind="Internal").ap()
    SPAN = -(-M // SETS)
    aggr = nc.dram_tensor("gat_sums", (SETS * RW, SPAN), F32, kind="Internal").ap()
    ident = k["ident"]
    both = range(LANES)
    by_token = lambda ap: ap[0:M, :].rearrange("(t p) n -> p t n", p=TP)
    with ExitStack() as outer:
        ob = lambda n, s, d=F32: outer.enter_context(nc.sbuf_tensor("gt_" + n, s, d))
        src = ob("src", [TP, TILES, SRC])
        bm = ob("bm", [TP, TILES, DST])
        top = ob("top", [TP, 4 * NHD])
        gates = ob("gates", [TP, TILES, NE])

        with ExitStack() as ctx:
            sb = lambda n, s, d=F32: ctx.enter_context(nc.sbuf_tensor("g1_" + n, s, d))
            w = sb("w", [C, HE])
            xs = [sb(f"xs{c}", [TP, NT, C]) for c in both]
            xT = [sb(f"xT{c}", [C, T]) for c in both]
            ps = [ctx.enter_context(nc.psum_tensor(f"g1_ps{c}", [128, 2, BANK], F32)) for c in both]
            load_all(nc, ctx, "g1", [(w[:, :], A["L3_ffn_W_gat"])], [(src[:, :, :], 1.0)])
            ch = Chain([ctx.enter_context(nc.semaphore(f"g1_step{c}")) for c in both], ["x", "turn", "xT", "feat", "out"])
            step, done = ch.sem, ch.after
            with nc.Block() as block:
                @block.sync
                def _(sp):
                    start_lanes(sp, ch)

                @block.tensor
                def _(pe):
                    with pe.Fori(0, PAIRS) as i:
                        for c in both:
                            pe.wait_ge(step[c], done(i, "x"))
                            pe.transpose(ps[c][:, 0, 0:TP], xs[c][:, :, :].rearrange("p t c -> p (t c)"),
                                         ident[0:TP, 0:TP]).then_inc(step[c], 1)
                        for c in both:
                            pe.wait_ge(step[c], done(i, "xT"))
                            for t in range(NT):
                                ins = pe.matmul(ps[c][0:TP, 1, t * HE:(t + 1) * HE], xT[c][:, t * TP:(t + 1) * TP], w[:, :], start=True, stop=True)
                            ins.then_inc(step[c], 1)

                @block.scalar
                def _(a):
                    with a.Fori(0, PAIRS) as i:
                        for c in both:
                            a.wait_ge(step[c], done(i, "turn"))
                            for t in range(NT):
                                ins = a.activation(xT[c][:, t * TP:(t + 1) * TP], ps[c][t * C:(t + 1) * C, 0, 0:TP], ACT.Copy)
                            ins.then_inc(step[c], 1)

                @block.vector
                def _(v):
                    with v.Fori(0, PAIRS) as i:
                        for c in both:
                            v.wait_ge(step[c], ch.before(i))
                            v.tensor_copy(xs[c][:, :, :], xn[:, bass.ds(i * (LANES * NT) + c * NT, NT), :]).then_inc(step[c], 1)
                        for c in both:
                            v.wait_ge(step[c], done(i, "feat"))
                            for t in range(NT):
                                tile = src[:, bass.ds(i * (LANES * NT) + (c * NT + t), 1), 0:RW]
                                ins = v.tensor_copy(tile.rearrange("p a (n e) -> p (a n) e", n=NHD)[:, :, 0:NE],
                                                    ps[c][0:TP, 1, t * HE:(t + 1) * HE].rearrange("p (n e) -> p n e", n=NHD))
                            ins.then_inc(step[c], 1)

        with ExitStack() as ctx:
            sb = lambda n, s, d=F32: ctx.enter_context(nc.sbuf_tensor("g2_" + n, s, d))
            att = sb("att", [TP, 2, HE])
            prod = sb("prod", [TP, TILES, HE])
            ext, row8 = sb("ext", [TP, 2 * NHD]), sb("row8", [2 * NHD, 1])
            diag, ones = sb("diag", [2 * NHD, 2 * NHD]), sb("ones", [2 * NHD, TP])
            ps = ctx.enter_context(nc.psum_tensor("g2_ps", [128, 2, BANK], F32))
            load_all(nc, ctx, "g2", [(att[:, q, :], row(A[f"L3_ffn_att_{n}"].rearrange("h e -> (h e)")).to_broadcast([TP, HE]))
                                     for q, n in enumerate(("src", "dst"))], [(ones[:, :], 1.0)])
            chain = Chain([ctx.enter_context(nc.semaphore("g2_step"))], [
                "src_prod", "src_sum", "dst_prod", "dst_sum", "max", "min", "negate", "turn", "all_max", "diag", "spread",
                "range_in", "range", "floor", "K", "inverse", "shift", "scale", "exp", "store:16"])
            s = chain.sem[0]
            after = lambda n: chain.after(0, n)
            a_, u_, b_ = src[:, :, RW:RW + NHD], src[:, :, RW + NHD:SRC], bm[:, :, 0:NHD]
            col = lambda q: top[:, q * NHD:(q + 1) * NHD]
            feats = src[:, :, 0:RW].rearrange("p t (n e) -> p t n e", n=NHD)[:, :, :, 0:NE]
            split = lambda ap: ap.rearrange("p t (n e) -> p t n e", n=NHD)
            with nc.Block() as block:
                @block.sync
                def _(sp):
                    sp.sem_inc(s, 1)
                    sp.wait_ge(s, after("exp"))
                    sp.dma_start(by_token(rows), src[:, :, :]).then_inc(s, 16)
                    sp.wait_ge(s, after("store"))

                @block.tensor
                def _(pe):
                    pe.wait_ge(s, after("negate"))
                    pe.matmul(ps[0:2 * NHD, 0, 0:TP], ext[:, :], ident[0:TP, 0:TP], start=True, stop=True).then_inc(s, 1)
                    pe.wait_ge(s, after("diag"))
                    pe.matmul(ps[0:TP, 1, 0:2 * NHD], ones[:, :], diag[:, :], start=True, stop=True).then_inc(s, 1)

                @block.scalar
                def _(a):
                    a.wait_ge(s, after("scale"))
                    a.activation(u_, u_, ACT.Exp).then_inc(s, 1)

                @block.vector
                def _(v):
                    v.wait_ge(s, 1)
                    last = None
                    for q, (name, dst) in enumerate((("src", a_), ("dst", b_))):
                        if last:
                            v.wait_ge(s, after(last))
                        weights = att[:, q, :].unsqueeze(1).to_broadcast([TP, TILES, HE])
                        for n in range(NHD):
                            ins = v.tensor_tensor(prod[:, :, n * NE:(n + 1) * NE], feats[:, :, n, :], weights[:, :, n * NE:(n + 1) * NE], ALU.mult)
                        ins.then_inc(s, 1)
                        v.wait_ge(s, after(name + "_prod"))
                        v.tensor_reduce(dst, split(prod[:, :, :]), AX.X, ALU.add).then_inc(s, 1)
                        last = name + "_sum"
                    v.wait_ge(s, after("dst_sum"))
                    v.tensor_reduce(ext[:, 0:NHD], a_.rearrange("p t n -> p n t"), AX.X, ALU.max).then_inc(s, 1)
                    v.wait_ge(s, after("max"))
                    v.tensor_reduce(ext[:, NHD:2 * NHD], a_.rearrange("p t n -> p n t"), AX.X, ALU.min).then_inc(s, 1)
                    v.wait_ge(s, after("min"))
                    v.tensor_scalar(ext[:, NHD:2 * NHD], ext[:, NHD:2 * NHD], -1.0, None, ALU.mult).then_inc(s, 1)
                    v.wait_ge(s, after("turn"))
                    v.tensor_reduce(row8[:, :], ps[0:2 * NHD, 0, 0:TP], AX.X, ALU.max).then_inc(s, 1)
                    v.wait_ge(s, after("all_max"))
                    v.tensor_scalar(diag[:, :], ident[0:2 * NHD, 0:2 * NHD], row8[:, :], None, ALU.mult).then_inc(s, 1)
                    v.wait_ge(s, after("spread"))
                    v.tensor_copy(top[:, 0:2 * NHD], ps[0:TP, 1, 0:2 * NHD]).then_inc(s, 1)
                    v.wait_ge(s, after("range_in"))
                    v.tensor_tensor(col(3), col(0), col(1), ALU.add).then_inc(s, 1)
                    v.wait_ge(s, after("range"))
                    v.tensor_scalar(col(3), col(3), RANGE, None, ALU.max).then_inc(s, 1)
                    v.wait_ge(s, after("floor"))
                    v.tensor_scalar(col(3), col(3), 1.0 / RANGE, None, ALU.mult).then_inc(s, 1)
                    v.wait_ge(s, after("K"))
                    v.reciprocal(col(2), col(3)).then_inc(s, 1)
                    v.wait_ge(s, after("inverse"))
                    v.tensor_tensor(u_, a_, repeat(col(0), TILES), ALU.subtract).then_inc(s, 1)
                    v.wait_ge(s, after("shift"))
                    v.tensor_tensor(u_, u_, repeat(col(2), TILES), ALU.mult).then_inc(s, 1)

        with ExitStack() as edges:
            eb = lambda n, s, d=F32: edges.enter_context(nc.sbuf_tensor("ed_" + n, s, d))
            srci, dsti = eb("srci", [128, CH], I32), eb("dsti", [128, CH], I32)
            lo, hi = eb("lo", [128, CH]), eb("hi", [128, CH])
            iota = eb("iota", [128, LO])
            zeros = eb("zeros", [128, BANK])
            with ExitStack() as ctx:
                bits = ctx.enter_context(nc.sbuf_tensor("ei_bits", [128, 2, CH], I32))
                load_all(nc, ctx, "ei", [
                    (srci[:, :], A["L3_ffn_edge_index"][0, :].rearrange("(p n) -> p n", p=128)),
                    (dsti[:, :], A["L3_ffn_edge_index"][1, :].rearrange("(p n) -> p n", p=128)),
                    (iota[:, :], k["iota"])], [(zeros[:, :], 0.0)])
                s = ctx.enter_context(nc.semaphore("ei_step"))
                with nc.Block() as block:
                    @block.vector
                    def _(v):
                        v.tensor_scalar(srci[:, :], srci[:, :], float(M - 1), None, ALU.min)
                        v.tensor_scalar(bits[:, 0, :], dsti[:, :], LO - 1, None, ALU.bitwise_and)
                        v.tensor_scalar(bits[:, 1, :], dsti[:, :], 7, None, ALU.arith_shift_right).then_inc(s, 1)
                        v.wait_ge(s, 1)
                        v.tensor_copy(lo[:, :], bits[:, 0, :])
                        v.tensor_copy(hi[:, :], bits[:, 1, :])
                        v.tensor_scalar(dsti[:, :], dsti[:, :], float(M - 1), None, ALU.min)

            EL, GS = 4, 8
            lanes = range(EL)
            with ExitStack() as ctx:
                sb = lambda n, s, d=F32: ctx.enter_context(nc.sbuf_tensor("g3_" + n, s, d))
                idx = [sb(f"idx{c}", [128, GS], I32) for c in lanes]
                got = [sb(f"got{c}", [128, GS, SRC]) for c in lanes]
                hot = [sb(f"hot{c}", [128, GS, LO]) for c in lanes]
                hih = [sb(f"hih{c}", [128, GS, HI]) for c in lanes]
                val = [sb(f"val{c}", [128, GS, HI, NHD]) for c in lanes]
                res = sb("res", [128, HI * NHD])
                ps = ctx.enter_context(nc.psum_tensor("g3_ps", [128, BANK], F32))
                opened, closed = ctx.enter_context(nc.semaphore("g3_opened")), ctx.enter_context(nc.semaphore("g3_closed"))
                stored = ctx.enter_context(nc.semaphore("g3_stored"))
                ch = Chain([ctx.enter_context(nc.semaphore(f"g3_step{c}")) for c in lanes],
                           ["idx", "store:16", "val", "add"])
                step, done = ch.sem, ch.after
                gathered = [ctx.enter_context(nc.semaphore(f"g3_gathered{c}")) for c in lanes]
                begun = ctx.enter_context(nc.semaphore("g3_gathers_begun"))
                first = lambda i, c: (i * EL + c) * GS
                with nc.Block() as block:
                    @block.gpsimd
                    def _(g):
                        with g.Fori(0, CH // (EL * GS)) as i:
                            for c in lanes:
                                g.wait_ge(step[c], done(i, "idx"))
                                g.sem_inc(begun, 1)
                                for n in range(GS):
                                    g.indirect_dma_start(got[c][:, n, :], None, rows, bass.IndirectOffsetOnAxis(
                                        ap=idx[c][:, n:n + 1].bitcast(U32), axis=0)).then_inc(gathered[c], 16)

                    @block.sync
                    def _(sp):
                        start_lanes(sp, ch)
                        with sp.Fori(0, CH // (EL * GS)) as i:
                            for c in lanes:
                                sp.wait_ge(gathered[c], i * (16 * GS) + 16 * GS)
                                sp.dma_start(kept[:, bass.ds(first(i, c), GS), :], got[c][:, :, :]).then_inc(step[c], 16)
                        for c in lanes:
                            sp.wait_ge(step[c], ch.before(CH // (EL * GS)))
                        sp.wait_ge(closed, 2)
                        sp.dma_start(csum.rearrange("(a p) n -> p a n", p=LO), res[:, :].rearrange("p (a n) -> p a n", n=NHD)).then_inc(stored, 16)
                        sp.wait_ge(stored, 16)

                    @block.tensor
                    def _(pe):
                        pe.matmul(ps[:, 0:HI * NHD], ident[:, :], zeros[:, 0:HI * NHD], start=True, stop=False, skip_group_check=True)
                        with pe.Fori(0, CH // (EL * GS)) as i:
                            for c in lanes:
                                pe.wait_ge(step[c], done(i, "val"))
                                for n in range(GS):
                                    ins = pe.matmul(ps[:, 0:HI * NHD], hot[c][:, n, :], val[c][:, n, :, :].rearrange("p a n -> p (a n)"),
                                                    start=False, stop=False, skip_group_check=True)
                                ins.then_inc(step[c], 1)
                        pe.matmul(ps[:, 0:HI * NHD], ident[:, :], zeros[:, 0:HI * NHD], start=False, stop=True,
                                  skip_group_check=True).then_inc(closed, 1)

                    @block.vector
                    def _(v):
                        with v.Fori(0, CH // (EL * GS)) as i:
                            for c in lanes:
                                chunk = bass.ds(first(i, c), GS)
                                v.wait_ge(step[c], ch.before(i))
                                v.tensor_copy(idx[c][:, :], srci[:, chunk]).then_inc(step[c], 1)
                                v.tensor_tensor(hot[c][:, :, :], repeat(iota[:, :], GS), spread(lo[:, chunk], LO), ALU.is_equal)
                                v.tensor_tensor(hih[c][:, :, :], repeat(iota[:, 0:HI], GS), spread(hi[:, chunk], HI), ALU.is_equal).then_inc(opened, 1)
                            for c in lanes:
                                v.wait_ge(opened, i * EL + (c + 1))
                                v.wait_ge(step[c], done(i, "store"))
                                u = got[c][:, :, RW + NHD:SRC]
                                v.tensor_tensor(val[c][:, :, :, :], spread(hih[c][:, :, :], NHD),
                                                u.unsqueeze(2).to_broadcast([128, GS, HI, NHD]), ALU.mult).then_inc(step[c], 1)
                        v.wait_ge(closed, 1)
                        v.tensor_copy(res[:, :], ps[:, 0:HI * NHD]).then_inc(closed, 1)

            with ExitStack() as ctx:
                cs = ctx.enter_context(nc.sbuf_tensor("g4_cs", [TP, TILES, NHD], F32))
                load_all(nc, ctx, "g4", [(cs[:, :, :], by_token(csum))])
                chain = Chain([ctx.enter_context(nc.semaphore("g4_step"))], [
                    "self", "log", "scale", "shift", "plus_b", "leaky", "store:16"])
                s = chain.sem[0]
                after = lambda n: chain.after(0, n)
                with nc.Block() as block:
                    @block.vector
                    def _(v):
                        v.wait_ge(s, 1)
                        v.tensor_tensor(cs[:, :, :], cs[:, :, :], u_, ALU.add).then_inc(s, 1)
                        v.wait_ge(s, after("log"))
                        v.tensor_tensor(cs[:, :, :], cs[:, :, :], repeat(col(3), TILES), ALU.mult).then_inc(s, 1)
                        v.wait_ge(s, after("scale"))
                        v.tensor_tensor(cs[:, :, :], cs[:, :, :], repeat(col(0), TILES), ALU.add).then_inc(s, 1)
                        v.wait_ge(s, after("shift"))
                        v.tensor_tensor(cs[:, :, :], cs[:, :, :], b_, ALU.add).then_inc(s, 1)
                        v.wait_ge(s, after("plus_b"))
                        v.scalar_tensor_tensor(out=bm[:, :, NHD:DST], in0=cs[:, :, :], scalar=0.2, in1=cs[:, :, :],
                                               op0=ALU.mult, op1=ALU.max).then_inc(s, 1)

                    @block.scalar
                    def _(a):
                        a.wait_ge(s, after("self"))
                        a.activation(cs[:, :, :], cs[:, :, :], ACT.Ln).then_inc(s, 1)

                    @block.sync
                    def _(sp):
                        sp.sem_inc(s, 1)
                        sp.wait_ge(s, after("leaky"))
                        sp.dma_start(by_token(drows), bm[:, :, :]).then_inc(s, 16)
                        sp.wait_ge(s, after("store"))

            EL2, GS2 = 8, 4
            lanes2 = range(EL2)
            PAIRS2 = [(c, c + 1) for c in lanes2[::2]]
            NBK = -(-SPAN // BANK)
            CUT = -(-SPAN // NBK)
            BANKS = [(q * CUT, min(SPAN, (q + 1) * CUT)) for q in range(NBK)]
            with ExitStack() as ctx:
                sb = lambda n, s, d=F32: ctx.enter_context(nc.sbuf_tensor("g5_" + n, s, d))
                idx = [sb(f"idx{c}", [128, GS2], I32) for c in lanes2]
                got = [sb(f"got{c}", [128, GS2, SRC]) for c in lanes2]
                tgt = [sb(f"tgt{c}", [128, GS2, DST]) for c in lanes2]
                ee = [sb(f"ee{c}", [128, GS2, NHD]) for c in lanes2]
                msg = [sb(f"msg{c}", [128, GS2, RW]) for c in lanes2]
                rest = [sb(f"rest{c}", [128, GS2, RW]) for c in lanes2]
                part = [sb(f"part{c}", [128, GS2, PARTS, RW], BF16) for c in lanes2]
                own = [sb(f"own{c}", [128, GS2, PARTS, SETS], BF16) for c in lanes2]
                at = [sb(f"at{c}", [128, GS2]) for c in lanes2]
                hot = [sb(f"hot{c}", [128, GS2, SPAN], BF16) for c in lanes2]
                val = [sb(f"val{c}", [128, GS2 * PARTS, SETS, RW], BF16) for c in lanes2]
                wide, places = sb("wide", [128, SPAN]), sb("places", [128, SPAN], F16)
                res = wide[0:SETS * RW, :]
                ps = ctx.enter_context(nc.psum_tensor("g5_ps", [128, len(BANKS), BANK], F32))
                opened, closed = ctx.enter_context(nc.semaphore("g5_opened")), ctx.enter_context(nc.semaphore("g5_closed"))
                stored = ctx.enter_context(nc.semaphore("g5_stored"))
                ch = Chain([ctx.enter_context(nc.semaphore(f"g5_step{c}")) for c in lanes2],
                           ["idx", "get:16", "sum", "leaky", "less_m", "cap", "exp", "msg",
                            "part0", "rest0", "part1", "part2", "val", "add"])
                step, done = ch.sem, ch.after
                gathered = [ctx.enter_context(nc.semaphore(f"g5_gathered{c}")) for c in lanes2]
                begun = ctx.enter_context(nc.semaphore("g5_gathers_begun"))
                first = lambda i, c: (i * EL2 + c) * GS2
                N = CH // (EL2 * GS2)
                taken, cutting = ctx.enter_context(nc.semaphore("g5_places_taken")), ctx.enter_context(nc.semaphore("g5_set_step"))
                load_all(nc, ctx, "g5", [(wide[:, :], k["places"])])
                with nc.Block() as block:
                    @block.vector
                    def _(v):
                        v.tensor_copy(places[:, :], wide[:, :])
                        v.scalar_tensor_tensor(out=hi[:, :], in0=hi[:, :], scalar=float(LO), in1=lo[:, :],
                                               op0=ALU.mult, op1=ALU.add).then_inc(cutting, 1)
                        v.wait_ge(cutting, 1)
                        v.tensor_scalar(lo[:, :], hi[:, :], float(SPAN), None, ALU.is_ge).then_inc(cutting, 1)
                        for n in range(2, SETS + 1):
                            v.wait_ge(cutting, n)
                            v.scalar_tensor_tensor(out=lo[:, :], in0=hi[:, :], scalar=float(n * SPAN), in1=lo[:, :],
                                                   op0=ALU.is_ge, op1=ALU.add).then_inc(cutting, 1)
                        v.wait_ge(cutting, SETS + 1)
                        v.scalar_tensor_tensor(out=hi[:, :], in0=lo[:, :], scalar=-float(SPAN), in1=hi[:, :], op0=ALU.mult, op1=ALU.add)

                with nc.Block() as block:
                    @block.gpsimd
                    def _(g):
                        with g.Fori(0, N) as i:
                            for c in lanes2:
                                g.wait_ge(step[c], done(i, "idx"))
                                g.sem_inc(begun, 1)
                                for n in range(GS2):
                                    g.indirect_dma_start(tgt[c][:, n, :], None, drows, bass.IndirectOffsetOnAxis(
                                        ap=idx[c][:, n:n + 1].bitcast(U32), axis=0)).then_inc(gathered[c], 16)

                    @block.sync
                    def _(sp):
                        start_lanes(sp, ch)
                        with sp.Fori(0, N) as i:
                            for c in lanes2:
                                sp.wait_ge(step[c], done(i, "idx"))
                                sp.dma_start(got[c][:, :, :], kept[:, bass.ds(first(i, c), GS2), :]).then_inc(step[c], 16)
                        sp.wait_ge(closed, 2)
                        sp.dma_start(aggr, res).then_inc(stored, 16)
                        sp.wait_ge(stored, 16)

                    @block.tensor
                    def _(pe):
                        for q, (a0, a1) in enumerate(BANKS):
                            pe.matmul(ps[0:SETS * RW, q, 0:a1 - a0], ident[:, 0:SETS * RW], zeros[:, 0:a1 - a0], start=True, stop=False,
                                      skip_group_check=True)
                        with pe.Fori(0, N) as i:
                            for c in lanes2:
                                pe.wait_ge(step[c], done(i, "val"))
                                for n in range(GS2 * PARTS):
                                    for q, (a0, a1) in enumerate(BANKS):
                                        ins = pe.matmul(ps[0:SETS * RW, q, 0:a1 - a0], val[c][:, n, :, :].rearrange("p a n -> p (a n)"),
                                                        hot[c][:, n // PARTS, a0:a1], start=False, stop=False, skip_group_check=True)
                                ins.then_inc(step[c], 1)
                        for q, (a0, a1) in enumerate(BANKS):
                            ins = pe.matmul(ps[0:SETS * RW, q, 0:a1 - a0], ident[:, 0:SETS * RW], zeros[:, 0:a1 - a0], start=False, stop=True,
                                            skip_group_check=True)
                        ins.then_inc(closed, 1)

                    @block.scalar
                    def _(a):
                        with a.Fori(0, N) as i:
                            for pair in PAIRS2:
                                for c in pair:
                                    a.wait_ge(step[c], done(i, "cap"))
                                    a.activation(ee[c][:, :, :], ee[c][:, :, :], ACT.Exp).then_inc(step[c], 1)
                                for n, (name, of) in enumerate((("msg", msg), ("rest0", rest))):
                                    for c in pair:
                                        a.wait_ge(step[c], done(i, name))
                                        a.activation(part[c][:, :, n, :], of[c][:, :, :], ACT.Copy).then_inc(step[c], 1)

                    @block.vector
                    def _(v):
                        with v.Fori(0, N) as i:
                            for pair in PAIRS2:
                                for c in pair:
                                    chunk = bass.ds(first(i, c), GS2)
                                    v.wait_ge(step[c], ch.before(i))
                                    v.tensor_copy(idx[c][:, :], dsti[:, chunk]).then_inc(step[c], 1)
                                    v.tensor_tensor(own[c][:, :, :, :], iota[:, 0:SETS].unsqueeze(1).unsqueeze(1).to_broadcast([128, GS2, PARTS, SETS]),
                                                    lo[:, chunk].unsqueeze(2).unsqueeze(2).to_broadcast([128, GS2, PARTS, SETS]), ALU.is_equal)
                                    v.tensor_copy(at[c][:, :], hi[:, chunk]).then_inc(taken, 1)
                                for c in pair:
                                    v.wait_ge(taken, i * EL2 + (c + 1))
                                    for n in range(GS2):
                                        ins = v.tensor_scalar(hot[c][:, n, :], places[:, :], at[c][:, n:n + 1], None, ALU.is_equal)
                                    ins.then_inc(opened, 1)
                                for c in pair:
                                    v.wait_ge(step[c], done(i, "get"))
                                    v.wait_ge(gathered[c], i * (16 * GS2) + 16 * GS2)
                                    v.tensor_tensor(ee[c][:, :, :], got[c][:, :, RW:RW + NHD], tgt[c][:, :, 0:NHD], ALU.add).then_inc(step[c], 1)
                                for c in pair:
                                    v.wait_ge(step[c], done(i, "sum"))
                                    v.scalar_tensor_tensor(out=ee[c][:, :, :], in0=ee[c][:, :, :], scalar=0.2, in1=ee[c][:, :, :],
                                                           op0=ALU.mult, op1=ALU.max).then_inc(step[c], 1)
                                for c in pair:
                                    v.wait_ge(step[c], done(i, "leaky"))
                                    v.tensor_tensor(ee[c][:, :, :], ee[c][:, :, :], tgt[c][:, :, NHD:DST], ALU.subtract).then_inc(step[c], 1)
                                for c in pair:
                                    v.wait_ge(step[c], done(i, "less_m"))
                                    v.tensor_scalar(ee[c][:, :, :], ee[c][:, :, :], 10.0, None, ALU.min).then_inc(step[c], 1)
                                for c in pair:
                                    v.wait_ge(step[c], done(i, "exp"))
                                    v.tensor_tensor(msg[c][:, :, :].rearrange("p g (n e) -> p (g n) e", n=NHD),
                                                    got[c][:, :, 0:RW].rearrange("p g (n e) -> p g n e", n=NHD),
                                                    spread(ee[c][:, :, :], NE + 1), ALU.mult).then_inc(step[c], 1)
                                for c in pair:
                                    v.wait_ge(step[c], done(i, "part0"))
                                    v.tensor_tensor(rest[c][:, :, :], msg[c][:, :, :], part[c][:, :, 0, :], ALU.subtract).then_inc(step[c], 1)
                                for c in pair:
                                    v.wait_ge(step[c], done(i, "part1"))
                                    v.tensor_tensor(part[c][:, :, 2, :], rest[c][:, :, :], part[c][:, :, 1, :], ALU.subtract).then_inc(step[c], 1)
                                for c in pair:
                                    v.wait_ge(opened, i * EL2 + (c + 1))
                                    v.wait_ge(step[c], done(i, "part2"))
                                    v.tensor_tensor(val[c][:, :, :, :], part[c][:, :, :, :].rearrange("p g k n -> p (g k) n").unsqueeze(2).to_broadcast(
                                        [128, GS2 * PARTS, SETS, RW]), spread(own[c][:, :, :, :].rearrange("p g k n -> p (g k) n"), RW),
                                        ALU.mult).then_inc(step[c], 1)
                        v.wait_ge(closed, 1)
                        for q, (a0, a1) in enumerate(BANKS):
                            ins = v.tensor_copy(res[:, a0:a1], ps[0:SETS * RW, q, 0:a1 - a0])
                        ins.then_inc(closed, 1)

        with ExitStack() as ctx:
            sb = lambda n, s, d=F32: ctx.enter_context(nc.sbuf_tensor("g6_" + n, s, d))
            ag = sb("ag", [TP, TILES, RW])
            agT = sb("agT", [RW, SETS, SPAN])
            PER = BANK // RW
            ps = ctx.enter_context(nc.psum_tensor("g6_ps", [128, -(-TILES // PER), BANK], F32))
            own = sb("own", [TP, TILES, NHD])
            vec = sb("vec", [TP, 3, HE])
            earlier = sb("earlier", [TP, NE, NE])
            z, zq = sb("z", [TP, TILES, HE]), sb("zq", [TP, TILES, HE])
            st = sb("st", [TP, 3, TILES])
            sc, gt, eq = sb("sc", [TP, TILES, NE]), sb("gt", [TP, TILES, NE, NE]), sb("eq", [TP, TILES, NE, NE])
            flat = lambda n: row(A["L3_ffn_" + n]).to_broadcast([TP, HE])
            load_all(nc, ctx, "g6", [(agT[:, :, :], aggr.rearrange("(a n) w -> n a w", n=RW)), (vec[:, 0, :], flat("b_gat")), (vec[:, 1, :], flat("ln_gamma")),
                                     (vec[:, 2, :], flat("ln_beta")), (earlier[:, :, :], k["earlier"])])
            names = ["turn", "sums", "e", "leaky", "less_m", "cap", "exp", "self", "sum", "inv", "norm", "bias", "mean_s", "mean", "centre",
                     "square", "var_s", "var", "std", "rstd", "unit", "gamma", "beta", "score", "quarter", "compare", "ties", "beats", "rank",
                     "chosen", "max", "less", "w_exp", "w", "w_sum", "w_inv", "gates"]
            chain = Chain([ctx.enter_context(nc.semaphore("g6_step"))], names)
            s = chain.sem[0]
            after = lambda n: chain.after(0, n)
            mean, var, rstd = (st[:, q, :] for q in range(3))
            heads = lambda ap, e: ap.rearrange("p t (n e) -> p t n e", e=e)
            with nc.Block() as block:
                @block.sync
                def _(sp):
                    sp.sem_inc(s, 1)

                @block.tensor
                def _(pe):
                    pe.wait_ge(s, 1)
                    flat_T = agT[:, :, :].rearrange("n a w -> n (a w)")
                    for t in range(TILES):
                        ins = pe.matmul(ps[0:TP, t // PER, (t % PER) * RW:(t % PER + 1) * RW], flat_T[:, t * TP:(t + 1) * TP],
                                        ident[0:RW, 0:RW], start=True, stop=True)
                    ins.then_inc(s, 1)

                @block.scalar
                def _(a):
                    a.wait_ge(s, after("cap"))
                    a.activation(own[:, :, :], own[:, :, :], ACT.Exp).then_inc(s, 1)
                    a.wait_ge(s, after("var"))
                    a.activation(var, var, ACT.Sqrt).then_inc(s, 1)
                    a.wait_ge(s, after("less"))
                    a.activation(sc[:, :, :], sc[:, :, :], ACT.Exp).then_inc(s, 1)

                @block.vector
                def _(v):
                    def stt(out, in0, scalar, in1, op0, op1):
                        return v.scalar_tensor_tensor(out=out, in0=in0, scalar=scalar, in1=in1, op0=op0, op1=op1)

                    tt, ts, red = v.tensor_tensor, v.tensor_scalar, v.tensor_reduce
                    own_, z_, zq_, sc_ = own[:, :, :], z[:, :, :], zq[:, :, :], sc[:, :, :]
                    gt_, eq_ = gt[:, :, :, :], eq[:, :, :, :]
                    v.wait_ge(s, after("turn"))
                    for q in range(-(-TILES // PER)):
                        n = min(PER, TILES - q * PER)
                        ins = v.tensor_copy(ag[:, q * PER:q * PER + n, :].rearrange("p t n -> p (t n)"), ps[0:TP, q, 0:n * RW])
                    ins.then_inc(s, 1)
                    v.wait_ge(s, after("sums"))
                    tt(own_, a_, b_, ALU.add).then_inc(s, 1)
                    v.wait_ge(s, after("e"))
                    stt(own_, own_, 0.2, own_, ALU.mult, ALU.max).then_inc(s, 1)
                    v.wait_ge(s, after("leaky"))
                    tt(own_, own_, bm[:, :, NHD:DST], ALU.subtract).then_inc(s, 1)
                    v.wait_ge(s, after("less_m"))
                    ts(own_, own_, 10.0, None, ALU.min).then_inc(s, 1)
                    v.wait_ge(s, after("exp"))
                    for n in range(NHD):
                        cut = slice(n * (NE + 1), (n + 1) * (NE + 1))
                        ins = tt(src[:, :, cut], src[:, :, cut], spread(own[:, :, n], NE + 1), ALU.mult)
                    ins.then_inc(s, 1)
                    v.wait_ge(s, after("self"))
                    tt(ag[:, :, :], ag[:, :, :], src[:, :, 0:RW], ALU.add).then_inc(s, 1)
                    den = heads(ag[:, :, :], NE + 1)[:, :, :, NE]
                    v.wait_ge(s, after("sum"))
                    v.reciprocal(own_, den).then_inc(s, 1)
                    v.wait_ge(s, after("inv"))
                    for n in range(NHD):
                        ins = tt(z[:, :, n * NE:(n + 1) * NE], ag[:, :, n * (NE + 1):n * (NE + 1) + NE], spread(own[:, :, n], NE), ALU.mult)
                    ins.then_inc(s, 1)
                    v.wait_ge(s, after("norm"))
                    tt(z_, z_, repeat(vec[:, 0, :], TILES), ALU.add).then_inc(s, 1)
                    v.wait_ge(s, after("bias"))
                    red(mean, z_, AX.X, ALU.add).then_inc(s, 1)
                    v.wait_ge(s, after("mean_s"))
                    ts(mean, mean, 1.0 / HE, None, ALU.mult).then_inc(s, 1)
                    v.wait_ge(s, after("mean"))
                    tt(z_, z_, spread(mean, HE), ALU.subtract).then_inc(s, 1)
                    v.wait_ge(s, after("centre"))
                    tt(zq_, z_, z_, ALU.mult).then_inc(s, 1)
                    v.wait_ge(s, after("square"))
                    red(var, zq_, AX.X, ALU.add).then_inc(s, 1)
                    v.wait_ge(s, after("var_s"))
                    ts(var, var, 1.0 / HE, 1e-5, ALU.mult, ALU.add).then_inc(s, 1)
                    v.wait_ge(s, after("std"))
                    v.reciprocal(rstd, var).then_inc(s, 1)
                    v.wait_ge(s, after("rstd"))
                    tt(z_, z_, spread(rstd, HE), ALU.mult).then_inc(s, 1)
                    v.wait_ge(s, after("unit"))
                    tt(z_, z_, repeat(vec[:, 1, :], TILES), ALU.mult).then_inc(s, 1)
                    v.wait_ge(s, after("gamma"))
                    tt(z_, z_, repeat(vec[:, 2, :], TILES), ALU.add).then_inc(s, 1)
                    v.wait_ge(s, after("beta"))
                    red(sc_, heads(z_, NE).rearrange("p t n e -> p t e n"), AX.X, ALU.add).then_inc(s, 1)
                    v.wait_ge(s, after("score"))
                    ts(sc_, sc_, 1.0 / NHD, None, ALU.mult).then_inc(s, 1)
                    other = sc_.unsqueeze(2).to_broadcast([TP, TILES, NE, NE])
                    v.wait_ge(s, after("quarter"))
                    tt(gt_, other, spread(sc_, NE), ALU.is_gt)
                    tt(eq_, other, spread(sc_, NE), ALU.is_equal).then_inc(s, 1)
                    v.wait_ge(s, after("compare"))
                    tt(eq_, eq_, earlier[:, :, :].unsqueeze(1).to_broadcast([TP, TILES, NE, NE]), ALU.mult).then_inc(s, 1)
                    v.wait_ge(s, after("ties"))
                    tt(gt_, gt_, eq_, ALU.add).then_inc(s, 1)
                    v.wait_ge(s, after("beats"))
                    red(gates[:, :, :], gt_, AX.X, ALU.add).then_inc(s, 1)
                    v.wait_ge(s, after("rank"))
                    ts(gates[:, :, :], gates[:, :, :], 2.0, None, ALU.is_lt).then_inc(s, 1)
                    v.wait_ge(s, after("chosen"))
                    red(mean, sc_, AX.X, ALU.max).then_inc(s, 1)
                    v.wait_ge(s, after("max"))
                    tt(sc_, sc_, spread(mean, NE), ALU.subtract).then_inc(s, 1)
                    v.wait_ge(s, after("w_exp"))
                    tt(gates[:, :, :], gates[:, :, :], sc_, ALU.mult).then_inc(s, 1)
                    v.wait_ge(s, after("w"))
                    red(mean, gates[:, :, :], AX.X, ALU.add).then_inc(s, 1)
                    v.wait_ge(s, after("w_sum"))
                    v.reciprocal(rstd, mean).then_inc(s, 1)
                    v.wait_ge(s, after("w_inv"))
                    tt(gates[:, :, :], gates[:, :, :], spread(rstd, NE), ALU.mult).then_inc(s, 1)

        with ExitStack() as ctx:
            sb = lambda n, s, d=F32: ctx.enter_context(nc.sbuf_tensor("f3_" + n, s, d))
            CA, HD = C + 1, 2 * C
            w1, w2, b2 = sb("w1", [CA, NE, HD]), sb("w2", [HD, NE, C]), sb("b2", [TP, NE * C])
            xs = [sb(f"xs{c}", [TP, NT, C]) for c in both]
            xT = [sb(f"xT{c}", [CA, T]) for c in both]
            hid = [sb(f"hid{c}", [HD, NE, T]) for c in both]
            y = [sb(f"y{c}", [TP, NT, NE, C]) for c in both]
            red_ = [sb(f"red{c}", [TP, NT, C]) for c in both]
            ps = [ctx.enter_context(nc.psum_tensor(f"f3_ps{c}", [128, 4, BANK], F32)) for c in both]
            load_all(nc, ctx, "f3", [
                (w1[0:C, :, :], A["L3_ffn_W1"].rearrange("e c n -> c e n")),
                (w1[C:CA, :, :].rearrange("p e n -> p (e n)"), row(A["L3_ffn_b1"].rearrange("e n -> (e n)"))),
                (w2[:, :, :], A["L3_ffn_W2"].rearrange("e n c -> n e c")),
                (b2[:, :], row(A["L3_ffn_b2"].rearrange("e c -> (e c)")).to_broadcast([TP, NE * C]))],
                [(xT[c][C:CA, :], 1.0) for c in both])
            ch = Chain([ctx.enter_context(nc.semaphore(f"f3_step{c}")) for c in both],
                       ["x", "turn", "xT", "hid", "gelu", "y", "bias", "weigh", "sum", "add"])
            step, done = ch.sem, ch.after
            with nc.Block() as block:
                @block.sync
                def _(sp):
                    start_lanes(sp, ch)

                @block.tensor
                def _(pe):
                    with pe.Fori(0, PAIRS) as i:
                        for c in both:
                            pe.wait_ge(step[c], done(i, "x"))
                            pe.transpose(ps[c][:, 0, 0:TP], xs[c][:, :, :].rearrange("p t c -> p (t c)"),
                                         ident[0:TP, 0:TP]).then_inc(step[c], 1)
                        for c in both:
                            pe.wait_ge(step[c], done(i, "xT"))
                            for n in range(NE):
                                ins = pe.matmul(ps[c][:, 1 + n // 2, (n % 2) * T:(n % 2 + 1) * T], w1[:, n, :], xT[c][:, :], start=True, stop=True)
                            ins.then_inc(step[c], 1)
                        for c in both:
                            pe.wait_ge(step[c], done(i, "gelu"))
                            for t in range(NT):
                                for n in range(NE):
                                    ins = pe.matmul(ps[c][0:TP, 3, (t * NE + n) * C:(t * NE + n + 1) * C], hid[c][:, n, t * TP:(t + 1) * TP],
                                                    w2[:, n, :], start=True, stop=True)
                            ins.then_inc(step[c], 1)

                @block.scalar
                def _(a):
                    with a.Fori(0, PAIRS) as i:
                        for c in both:
                            a.wait_ge(step[c], done(i, "turn"))
                            for t in range(NT):
                                ins = a.activation(xT[c][0:C, t * TP:(t + 1) * TP], ps[c][t * C:(t + 1) * C, 0, 0:TP], ACT.Copy)
                            ins.then_inc(step[c], 1)
                        for c in both:
                            a.wait_ge(step[c], done(i, "hid"))
                            a.activation(hid[c][:, :, :].rearrange("p (k n) w -> p k (n w)", k=2), ps[c][:, 1:3, 0:2 * T], ACT.Gelu).then_inc(step[c], 1)

                @block.vector
                def _(v):
                    with v.Fori(0, PAIRS) as i:
                        tiles = [bass.ds(i * (LANES * NT) + c * NT, NT) for c in both]
                        for c in both:
                            v.wait_ge(step[c], ch.before(i))
                            v.tensor_copy(xs[c][:, :, :], xn[:, tiles[c], :]).then_inc(step[c], 1)
                        for c in both:
                            v.wait_ge(step[c], done(i, "y"))
                            v.tensor_tensor(y[c][:, :, :, :].rearrange("p t e c -> p t (e c)"), ps[c][0:TP, 3, :].rearrange("p (t n) -> p t n", t=NT),
                                            repeat(b2[:, :], NT), ALU.add).then_inc(step[c], 1)
                        for c in both:
                            v.wait_ge(step[c], done(i, "bias"))
                            v.tensor_tensor(y[c][:, :, :, :], y[c][:, :, :, :], spread(gates[:, tiles[c], :], C), ALU.mult).then_inc(step[c], 1)
                        for c in both:
                            v.wait_ge(step[c], done(i, "weigh"))
                            v.tensor_reduce(red_[c][:, :, :], y[c][:, :, :, :].rearrange("p t e c -> p t c e"), AX.X, ALU.add).then_inc(step[c], 1)
                        for c in both:
                            v.wait_ge(step[c], done(i, "sum"))
                            v.tensor_tensor(h[:, tiles[c], :], h[:, tiles[c], :], red_[c][:, :, :], ALU.add).then_inc(step[c], 1)


def constants():
    i = (np.arange(NT)[:, None] * TP + np.arange(TP)[None, :]).T
    j = np.arange(T)
    strict = np.where(j[None, None, :] < i[:, :, None], 0.0, NEG)
    causal = np.where(j[None, None, :] <= i[:, :, None], 0.0, NEG)
    window = np.where((j[None, None, :] <= i[:, :, None]) & (i[:, :, None] - j[None, None, :] <= 128), 0.0, NEG)
    before = (j[None, None, :] < i[:, :, None]) * 1.0
    own = (j[None, None, :] == i[:, :, None]) * 1.0
    d = np.arange(C)
    freq = 10000.0 ** (-2.0 * np.arange(C // 2) / C)
    theta = (j[:, None].astype(np.float32) * freq[None, :].astype(np.float32)).astype(np.float32)
    cos, sin = np.cos(theta.astype(np.float64)), np.sin(theta.astype(np.float64))
    rope = np.concatenate([cos[:, d // 2].T, (sin[:, d // 2] * np.where(d % 2, 1.0, -1.0)).T])
    fold = (np.arange(128)[:, None] % C == np.arange(128)[None, :] % C) * 1.0
    r, p = np.arange(96)[:, None], np.arange(128)[None, :]
    picks = np.stack([r % 32 == 4 * n + p // 32 for n in range(8)] + [r % 32 == p % 32], 1) * 1.0
    out = {
        "picks": picks, "ident": np.eye(128), "strict": strict, "causal": causal, "window": window, "before": before,
        "own": own, "rope": rope, "fold": fold, "valid": (i > 0) * 1.0,
        "earlier": np.tile((np.arange(4)[None, :] < np.arange(4)[:, None]) * 1.0, (TP, 1, 1)),
        "iota": np.tile(np.arange(128.0), (128, 1)),
        "places": np.tile(np.arange(-(-M // 6) * 1.0), (128, 1)),
    }
    return {n: np.ascontiguousarray(a.astype(np.float32)) for n, a in out.items()}


def layouts(I):
    D = {n: np.ascontiguousarray(a) for n, a in I.items() if n not in ("x", "L0_ffn_attention_mask")}
    D["xT"] = np.ascontiguousarray(np.transpose(I["x"], (0, 2, 1)).reshape(B // 2, 2 * C, L))

    def heads_t(w, b=None, n=8):
        w = w if b is None else np.concatenate([w, b[None, :]], 0)
        return np.ascontiguousarray(np.transpose(w.reshape(w.shape[0], n, -1), (2, 1, 0)))

    for w in "qkv":
        D["L0_attn_W" + w + "T"] = heads_t(I["L0_attn_W" + w], I["L0_attn_b" + w])
    D["L0_attn_WuH"] = np.ascontiguousarray(np.transpose(I["L0_attn_Wu"].reshape(8, C, C), (1, 0, 2)))
    for n, w in enumerate("qkv"):
        part = I["L3_attn_W_qkv"][n * 256:(n + 1) * 256]
        D["L3_attn_W" + w + "H"] = np.ascontiguousarray(np.transpose(part.reshape(8, 32, C), (1, 0, 2)))
    D["L3_attn_WvT"] = np.ascontiguousarray(part.T)
    D["L3_attn_WgT"] = np.ascontiguousarray(I["L3_attn_W_gate"].T)
    D["L3_attn_WfT"] = np.ascontiguousarray(I["L3_attn_W_final"].T)
    swap = np.arange(C) ^ 1
    q = np.transpose(I["L1_attn_wq"].reshape(16, C, C), (2, 0, 1))
    D["L1_attn_wq2"] = np.ascontiguousarray(np.concatenate([q, q[:, :, swap]], 2))
    D["L1_attn_wqT"] = np.ascontiguousarray(q.reshape(C, 16 * C))
    kT = I["L1_attn_wkv"][0:C].T
    D["L1_attn_wk2"] = np.ascontiguousarray(np.concatenate([kT, kT[:, swap]], 1))
    D["L1_attn_woH"] = np.ascontiguousarray(np.transpose(I["L1_attn_wo"].reshape(C, 16, C), (2, 1, 0)).reshape(C, 16 * C))
    D["L2_attn_WqkvH"] = np.ascontiguousarray(np.transpose(I["L2_attn_Wqkv"].reshape(C, 3, C, 8), (0, 1, 3, 2)).reshape(C, -1))
    D["L2_attn_bqkvH"] = np.ascontiguousarray(np.transpose(I["L2_attn_bqkv"].reshape(3, C, 8), (0, 2, 1)).reshape(-1))
    D["L2_attn_W0H"] = np.ascontiguousarray(np.transpose(I["L2_attn_W0"].reshape(C, 8, C), (1, 0, 2)).reshape(-1, C))
    kv = np.concatenate([I["L2_ffn_keys_table"], I["L2_ffn_values_table"]], 1).reshape(8, 16, 4, 2, 32, 2 * C)
    D["L2_ffn_tables"] = np.ascontiguousarray(np.transpose(kv, (0, 2, 4, 1, 3, 5))).reshape(8, 128, 32, 2 * C)
    D["L2_ffn_WpkT"] = np.ascontiguousarray(np.transpose(I["L2_ffn_Wq_pk"].reshape(C, 2, 8, 32), (1, 3, 2, 0)).reshape(C, 8, C))
    D["L2_ffn_pkT"] = np.ascontiguousarray(np.transpose(I["L2_ffn_pk_keys"], (0, 3, 2, 1)))
    D["L2_ffn_WoH"] = np.ascontiguousarray(I["L2_ffn_Wo"].reshape(8, C, C))
    return D


def build(nc, A, out, K, first=0, last=9, h_in=None):
    with ExitStack() as ctx:
        h = ctx.enter_context(nc.sbuf_tensor("h", [TP, TILES, C], F32))
        xn = ctx.enter_context(nc.sbuf_tensor("xn", [TP, TILES, C], F32))
        k = {n: ctx.enter_context(nc.sbuf_tensor("k_" + n, list(K[n].shape), F32)) for n in ("ident",)}
        load_all(nc, ctx, "k", [(k["ident"][:, :], K["ident"])])
        if h_in is not None:
            load_all(nc, ctx, "hin", [(h[:, :, :], h_in.rearrange("b (t p) c -> p (b t) c", p=TP))])
        K = {**K, **k}
        stages = [stage_tok, stage_l0_attn, stage_l0_ffn, stage_l1_attn, stage_l1_ffn, stage_l2_attn, stage_l2_ffn,
                  stage_l3_attn, stage_l3_ffn]
        for n in range(first, last):
            if n:
                layernorm_all(nc, h, xn, f"s{n}")
                stages[n](nc, h, xn, K, A)
            else:
                stages[n](nc, h, K, A)
        stored = ctx.enter_context(nc.semaphore("stored"))
        with nc.Block() as block:
            @block.sync
            def _(sp):
                sp.dma_start(out.rearrange("b (t p) c -> p (b t) c", p=TP), h[:, :, :]).then_inc(stored, 16)
                sp.wait_ge(stored, 16)


def kernel(**inputs):
    import concourse.bacc as bacc
    from concourse.bass_utils import run_bass_kernel_spmd

    nc = bacc.Bacc("TRN2", target_bir_lowering=False, num_devices=1)
    arrays, A, K = {}, {}, {}
    for table, of in ((A, layouts({n: np.asarray(a) for n, a in inputs.items()})), (K, constants())):
        for name, a in of.items():
            arrays[f"in_{name}"] = a
            table[name] = nc.dram_tensor(f"in_{name}", a.shape, mybir.dt.from_np(a.dtype), kind="ExternalInput").ap()
    out = nc.dram_tensor("out_0", (B, T, C), F32, kind="ExternalOutput").ap()
    build(nc, A, out, K)
    r = run_bass_kernel_spmd(nc, [arrays], core_ids=[0])
    return r.results[0]["out_0"]
```
